# Optimizing a Trainium2 kernel written in Bass

```python
import numpy as np
import jax
import jax.numpy as jnp

def _softmax(x, axis=-1):
    return jax.nn.softmax(x, axis=axis)

def _gelu(x):
    return jax.nn.gelu(x, approximate=True)

def _silu(x):
    return jax.nn.silu(x)

def _sigmoid(x):
    return jax.nn.sigmoid(x)

def _layernorm(x, axis=-1, eps=1e-05):
    m = jnp.mean(x, axis=axis, keepdims=True)
    v = jnp.var(x, axis=axis, keepdims=True)
    return (x - m) / jnp.sqrt(v + eps)

def _scatter_add(tgt, idx, src, axis=0):
    return tgt.at[idx].add(src)

def _segment_sum(src, seg, n):
    return jax.ops.segment_sum(src, seg, n)
kernel_name = 'mk_conv_seq_d2_conv_nhwc512_r4_353f43'

def setup_inputs(seed: int=0):
    np.random.seed(seed)
    _w = jnp.asarray

    def _rec_inputs():
        import jax
        import jax.numpy as jnp
        _gk = jax.random.key(seed)
        x = -0.0003929 + 0.9999 * jax.random.normal(jax.random.fold_in(_gk, 1), (8, 16, 16, 128), jnp.float32)
        return x
    x = _rec_inputs()

    def _L0_conv_setup():
        import jax, jax.numpy as jnp
        import numpy as np
        B, H, W, C = (8, 16, 16, 128)
        G = 32
        EPS = 1e-05

        def group_norm(x, scale, bias):
            b, h, w, c = x.shape
            xg = x.reshape(b, h, w, G, c // G)
            mean = jnp.mean(xg, axis=(1, 2, 4), keepdims=True)
            var = jnp.var(xg, axis=(1, 2, 4), keepdims=True)
            xg = (xg - mean) / jnp.sqrt(var + EPS)
            x = xg.reshape(b, h, w, c)
            return x * scale + bias

        def conv1x1(x, w, b):
            return jnp.einsum('bhwc,cd->bhwd', x, w) + b
        key = jax.random.key(seed)
        ks = jax.random.split(key, 10)
        init = lambda k, shape: jax.random.normal(k, shape, dtype=jnp.float32) * (1.0 / np.sqrt(C))
        return {'x': jax.random.normal(ks[0], (B, H, W, C), dtype=jnp.float32), 'gn_scale': jnp.ones((C,), dtype=jnp.float32), 'gn_bias': jnp.zeros((C,), dtype=jnp.float32), 'wq': init(ks[1], (C, C)), 'bq': jnp.zeros((C,), jnp.float32), 'wk': init(ks[2], (C, C)), 'bk': jnp.zeros((C,), jnp.float32), 'wv': init(ks[3], (C, C)), 'bv': jnp.zeros((C,), jnp.float32), 'wo': init(ks[4], (C, C)), 'bo': jnp.zeros((C,), jnp.float32)}
    _L0_conv_all = _L0_conv_setup()
    _L0_conv_in = {k: v for k, v in _L0_conv_all.items() if k in ('gn_scale', 'gn_bias', 'wq', 'bq', 'wk', 'bk', 'wv', 'bv', 'wo', 'bo')}
    del _L0_conv_all

    def _L1_conv_setup():
        import jax, jax.numpy as jnp
        import numpy as np
        N, H, W, C, HEADS = (8, 16, 16, 128, 8)
        HD = C // HEADS
        key = jax.random.key(seed)
        ks = jax.random.split(key, 5)
        x = jax.random.normal(ks[0], (N, H, W, C), dtype=jnp.float32)
        w_qkv = jax.random.normal(ks[1], (C, 3 * C), dtype=jnp.float32) / np.sqrt(C)
        b_qkv = jnp.zeros((3 * C,), dtype=jnp.float32)
        w_out = jax.random.normal(ks[2], (C, C), dtype=jnp.float32) / np.sqrt(C)
        b_out = jnp.zeros((C,), dtype=jnp.float32)
        gamma = jnp.ones((1, 1, 1, C), dtype=jnp.float32)
        beta = jnp.zeros((1, 1, 1, C), dtype=jnp.float32)
        return {'x': x, 'w_qkv': w_qkv, 'b_qkv': b_qkv, 'w_out': w_out, 'b_out': b_out, 'gamma': gamma, 'beta': beta}
    _L1_conv_all = _L1_conv_setup()
    _L1_conv_in = {k: v for k, v in _L1_conv_all.items() if k in ('w_qkv', 'b_qkv', 'w_out', 'b_out', 'gamma', 'beta')}
    del _L1_conv_all
    return {'x': x, 'L0_conv_gn_scale': _L0_conv_in['gn_scale'], 'L0_conv_gn_bias': _L0_conv_in['gn_bias'], 'L0_conv_wq': _L0_conv_in['wq'], 'L0_conv_bq': _L0_conv_in['bq'], 'L0_conv_wk': _L0_conv_in['wk'], 'L0_conv_bk': _L0_conv_in['bk'], 'L0_conv_wv': _L0_conv_in['wv'], 'L0_conv_bv': _L0_conv_in['bv'], 'L0_conv_wo': _L0_conv_in['wo'], 'L0_conv_bo': _L0_conv_in['bo'], 'L1_conv_w_qkv': _L1_conv_in['w_qkv'], 'L1_conv_b_qkv': _L1_conv_in['b_qkv'], 'L1_conv_w_out': _L1_conv_in['w_out'], 'L1_conv_b_out': _L1_conv_in['b_out'], 'L1_conv_gamma': _L1_conv_in['gamma'], 'L1_conv_beta': _L1_conv_in['beta']}

def reference(x, L0_conv_gn_scale, L0_conv_gn_bias, L0_conv_wq, L0_conv_bq, L0_conv_wk, L0_conv_bk, L0_conv_wv, L0_conv_bv, L0_conv_wo, L0_conv_bo, L1_conv_w_qkv, L1_conv_b_qkv, L1_conv_w_out, L1_conv_b_out, L1_conv_gamma, L1_conv_beta):
    import jax
    import jax.numpy as jnp

    def _L0_conv_ref(x, gn_scale, gn_bias, wq, bq, wk, bk, wv, bv, wo, bo):
        import jax, jax.numpy as jnp
        import numpy as np
        B, H, W, C = (8, 16, 16, 128)
        G = 32
        EPS = 1e-05

        def group_norm(x, scale, bias):
            b, h, w, c = x.shape
            xg = x.reshape(b, h, w, G, c // G)
            mean = jnp.mean(xg, axis=(1, 2, 4), keepdims=True)
            var = jnp.var(xg, axis=(1, 2, 4), keepdims=True)
            xg = (xg - mean) / jnp.sqrt(var + EPS)
            x = xg.reshape(b, h, w, c)
            return x * scale + bias

        def conv1x1(x, w, b):
            return jnp.einsum('bhwc,cd->bhwd', x, w) + b
        h = group_norm(x, gn_scale, gn_bias)
        q = conv1x1(h, wq, bq)
        k = conv1x1(h, wk, bk)
        v = conv1x1(h, wv, bv)
        b, hh, ww, c = h.shape
        n = hh * ww
        q = q.reshape(b, n, c)
        k = k.reshape(b, n, c)
        v = v.reshape(b, n, c)
        scores = jnp.einsum('bqc,bkc->bqk', q, k) * c ** (-0.5)
        attn = jax.nn.softmax(scores, axis=-1)
        out = jnp.einsum('bqk,bkc->bqc', attn, v).reshape(b, hh, ww, c)
        out = conv1x1(out, wo, bo)
        return out + x

    def _L1_conv_ref(x, w_qkv, b_qkv, w_out, b_out, gamma, beta):
        import jax, jax.numpy as jnp
        import numpy as np
        N, H, W, C, HEADS = (8, 16, 16, 128, 8)
        HD = C // HEADS
        n, h, w, c = x.shape
        heads, hd = (HEADS, c // HEADS)
        L = h * w
        identity = x
        qkv = jnp.einsum('nhwc,cd->nhwd', x, w_qkv) + b_qkv
        qkv = qkv.reshape(n, h, w, 3, heads, hd).transpose(3, 0, 4, 1, 2, 5)
        q, k, v = (qkv[0], qkv[1], qkv[2])
        q = q.reshape(n, heads, L, hd)
        k = k.reshape(n, heads, L, hd)
        v = v.reshape(n, heads, L, hd)
        q = jax.nn.softmax(q, axis=-1)
        k = jax.nn.softmax(k, axis=-2)
        context = jnp.einsum('nelk,neld->nekd', k, v)
        out = jnp.einsum('nekd,nelk->neld', context, q)
        out = out.reshape(n, heads, h, w, hd).transpose(0, 2, 3, 1, 4).reshape(n, h, w, c)
        out = jnp.einsum('nhwc,cd->nhwd', out, w_out) + b_out
        out = out * jax.nn.sigmoid(gamma) + beta
        return identity + out

    def _gn(v, G=32, eps=1e-05):
        B_, H_, W_, C_ = v.shape
        g = v.reshape(B_, H_, W_, G, C_ // G)
        m = jnp.mean(g, axis=(1, 2, 4), keepdims=True)
        s = jnp.var(g, axis=(1, 2, 4), keepdims=True)
        return ((g - m) / jnp.sqrt(s + eps)).reshape(v.shape)

    def _ln_c(v, eps=1e-06):
        m = jnp.mean(v, axis=-1, keepdims=True)
        s = jnp.var(v, axis=-1, keepdims=True)
        return (v - m) / jnp.sqrt(s + eps)

    def _ln_t(v, eps=1e-05):
        m = jnp.mean(v, axis=-1, keepdims=True)
        s = jnp.var(v, axis=-1, keepdims=True)
        return (v - m) / jnp.sqrt(s + eps)

    def _to_tokens(v):
        B_, H_, W_, C_ = v.shape
        return v.reshape(B_, H_ * W_, C_)

    def _from_tokens(t, like):
        return t.reshape(like.shape)
    x = _L0_conv_ref(x, L0_conv_gn_scale, L0_conv_gn_bias, L0_conv_wq, L0_conv_bq, L0_conv_wk, L0_conv_bk, L0_conv_wv, L0_conv_bv, L0_conv_wo, L0_conv_bo)
    x = _L1_conv_ref(x, L1_conv_w_qkv, L1_conv_b_qkv, L1_conv_w_out, L1_conv_b_out, L1_conv_gamma, L1_conv_beta)
    return x

_drawn_inputs = setup_inputs


def setup_inputs(seed=0):
    import zlib

    import numpy as np

    out = dict(_drawn_inputs(seed))
    spreads = {'L0_conv_gn_scale': (1.0, 0.2),
     'L0_conv_gn_bias': (0.0, 0.1),
     'L0_conv_bq': (0.0, 0.605),
     'L0_conv_bk': (0.0, 0.8),
     'L0_conv_bv': (0.0, 0.1),
     'L0_conv_bo': (0.0, 0.1),
     'L1_conv_b_qkv': (0.0, 0.1),
     'L1_conv_b_out': (0.0, 0.1),
     'L1_conv_gamma': (1.0, 0.6),
     'L1_conv_beta': (0.0, 0.1)}
    factors = {}
    for name, (base, spread) in spreads.items():
        noise = np.random.default_rng([zlib.crc32(name.encode()), seed]).standard_normal(out[name].shape)
        drawn = base * np.exp(spread * noise) if base else spread * noise
        out[name] = jnp.asarray(drawn.astype(out[name].dtype))
    for name, factor in factors.items():
        out[name] = (out[name] * factor).astype(out[name].dtype)
    return out
```

```python
from contextlib import ExitStack

import concourse.bass as bass
from concourse import mybir

F32 = mybir.dt.float32
F32R = mybir.dt.float32r
ALU = mybir.AluOpType
ACT = mybir.ActivationFunctionType
AX_X = mybir.AxisListType.X

GROUPS = 32
HEADS = 8
EPS = 1e-05


def build(nc, x, gn_scale, gn_bias, wq, bq, wk, bk, wv, bv, wo, bo, w_qkv, b_qkv, w_out, b_out, gamma, beta, out):
    B, H, W, C = x.shape
    L = H * W
    P = 128
    J = L // P
    HD = C // HEADS
    GC = C // GROUPS
    SCALE = float(C) ** -0.5
    assert C == P and J == 2

    x_d = x.rearrange("b h w c -> b (h w) c").rearrange("b (p j) c -> b p (j c)", j=J)
    y_d = out.rearrange("b h w c -> b (h w) c").rearrange("b (p j) c -> b p (j c)", j=J)

    with ExitStack() as ctx:
        def sb(name, shape, dt=F32):
            return ctx.enter_context(nc.sbuf_tensor(name, shape, dt))

        def ps(name, shape):
            return ctx.enter_context(nc.psum_tensor(name, shape, F32))

        def sem(name):
            return ctx.enter_context(nc.semaphore(name))

        ident = sb("ident", [P, P])
        group_neg = sb("group_neg", [P, P])
        head_mask = sb("head_mask", [P, P])
        wq_s, wk_s, wv_s, wo_s = (sb(n, [P, C]) for n in ("wq_s", "wk_s", "wv_s", "wo_s"))
        wqT, wkT, wvT = (sb(n, [P, C]) for n in ("wqT", "wkT", "wvT"))
        w1 = sb("w1", [P, 3, C])
        w1_hi = sb("w1_hi", [P, 3, C], F32R)
        w1_lo = sb("w1_lo", [P, 3, C], F32R)
        wout_s = sb("wout_s", [P, C])
        wout_sig = sb("wout_sig", [P, C])
        NVEC = 5
        GNS, GNB, BQ, BV, BV1 = range(NVEC)
        vec_rows = sb("vec_rows", [NVEC, C])
        vec = sb("vec", [P, NVEC])
        bo_b, bq1_b, gamma_b, beta_b, bout_b = (sb(n, [P, C]) for n in ("bo_b", "bq1_b", "gamma_b", "beta_b", "bout_b"))
        a_f = sb("a_f", [P, C])
        a_hi = sb("a_hi", [P, C], F32R)
        a_lo = sb("a_lo", [P, C], F32R)
        a_bias = sb("a_bias", [P, 1])
        wvo = sb("wvo", [P, C])
        bvb = sb("bvb", [P, C])
        bv1b = sb("bv1b", [P, C])
        val_bias = sb("val_bias", [P, C])
        y_bias = sb("y_bias", [P, C])
        sig = sb("sig", [P, C])
        sig_e = sb("sig_e", [P, C])
        sig_d = sb("sig_d", [P, C])
        yb_t = sb("yb_t", [P, C])
        yb_u = sb("yb_u", [P, C])
        neg_half = sb("neg_half", [P, B])

        x_all = sb("x_all", [P, B, J * C])
        xT_all = sb("xT_all", [P, B, L])
        x1b_all = sb("x1b_all", [P, B, J * C])
        y_all = sb("y_all", [P, B, J * C])
        stats = sb("stats", [P, B, 6])
        mv = sb("mv", [P, B, 2])
        neg_mean = sb("neg_mean", [P, B])
        dev = sb("dev", [P, B])
        dev2 = sb("dev2", [P, B])
        var_t = sb("var_t", [P, B])
        var_g = sb("var_g", [P, B])
        rstd = sb("rstd", [P, B])
        gn_a = sb("gn_a", [P, B])
        gn_ba = sb("gn_ba", [P, B])
        gn_b = sb("gn_b", [P, B])

        hT = sb("hT", [P, L])
        hT_hi = sb("hT_hi", [P, L], F32R)
        hT_lo = sb("hT_lo", [P, L], F32R)
        uT = sb("uT", [P, L])
        uT_hi = sb("uT_hi", [P, L], F32R)
        uT_lo = sb("uT_lo", [P, L], F32R)
        vals = sb("vals", [P, J, C + 1])
        neg_smax = sb("neg_smax", [P, J])
        probs = sb("probs", [P, J, L])
        probsT = sb("probsT", [P, J, L])
        inv_sum = sb("inv_sum", [P, J])
        x1 = sb("x1", [P, J * C])
        x1T_hi = sb("x1T_hi", [P, L], F32R)
        x1T_lo = sb("x1T_lo", [P, L], F32R)
        neg_kmax = sb("neg_kmax", [P, 1])
        kT_exp = sb("kT_exp", [P, L])
        k_sum = sb("k_sum", [P, 1])
        k_inv = sb("k_inv", [P, 1])
        k_exp = sb("k_exp", [P, J * C])
        v1 = sb("v1", [P, J, C])
        q_b = sb("q_b", [P, J, C])
        q_max = sb("q_max", [P, J * HEADS])
        q_sh = sb("q_sh", [P, J * C])
        q_exp = sb("q_exp", [P, J * C])
        q_sum = sb("q_sum", [P, J * HEADS])
        q_inv = sb("q_inv", [P, J * HEADS])
        q_sm = sb("q_sm", [P, J * C])
        qT = sb("qT", [P, L])
        ctxT = sb("ctxT", [P, C])
        m_s = sb("m_s", [P, C])

        b_ux = ps("b_ux", [P, 512])
        b_val = ps("b_val", [P, 512])
        b_s = ps("b_s", [P, 512])
        b_att = ps("b_att", [P, 512])
        b_qv = ps("b_qv", [P, 512])
        b_k = ps("b_k", [P, 512])
        b_q = ps("b_q", [P, 512])
        b_y = ps("b_y", [P, 512])
        u_ps, x1T_ps = b_ux[:, 0:L], b_ux[:, L:2 * L]
        val_ps = b_val[:, 0:J * C].rearrange("p (j c) -> p j c", j=J)
        s_ps = b_s[:, :].rearrange("p (j l) -> p j l", j=J)
        att_ps = b_att[:, 0:J * (C + 1)].rearrange("p (j c) -> p j c", j=J)
        qv_ps = b_qv[:, :].rearrange("p (j a c) -> p j a c", j=J, a=2)
        kT_ps, k_ps = b_k[:, 0:L], b_k[:, L:2 * L]
        qT_ps = b_q[:, 0:L]
        ctx_ps, m_ps, y_ps = b_y[:, 0:C], b_y[:, C:2 * C], b_y[:, 2 * C:2 * C + J * C]
        xT_ps = [b[:, 0:L] for b in (b_s, b_att, b_y, b_q)]
        wT_ps, fold_ps, stat_ps, bias1_ps = b_qv, b_ux, b_k, b_k

        x_in = [sem(f"x_in{b}") for b in range(B)]
        qkw_in, vw_in, w1_in, wout_in, vec_in, rows_in = (
            sem(n) for n in ("qkw_in", "vw_in", "w1_in", "wout_in", "vec_in", "rows_in"))
        ident_ready, masks_ready, pow_ready = sem("ident_ready"), sem("masks_ready"), sem("pow_ready")
        pool_set = sem("pool_set")
        xT_done, stats_done, xT_copied = sem("xT_done"), sem("stats_done"), sem("xT_copied")
        wT_done, wT_copied = sem("wT_done"), sem("wT_copied")
        dve_set = sem("dve_set")
        mv_ready, mean_done, dev_ready, var_done, var_ready = (
            sem(n) for n in ("mv_ready", "mean_done", "dev_ready", "var_done", "var_ready"))
        gn_ready, fold_done, a_copied, a_split, fold_ready, w1_split = (
            sem(n) for n in ("gn_ready", "fold_done", "a_copied", "a_split", "fold_ready", "w1_split"))
        sig_exp, wout_ready, bias1_done, y_bias_ready = (
            sem(n) for n in ("sig_exp", "wout_ready", "bias1_done", "y_bias_ready"))
        h_ready, h_hi_ready, h_lo_ready = sem("h_ready"), sem("h_hi_ready"), sem("h_lo_ready")
        u_done, u_ready, u_hi_ready, u_lo_ready = sem("u_done"), sem("u_ready"), sem("u_hi_ready"), sem("u_lo_ready")
        val_done, val_ready = sem("val_done"), sem("val_ready")
        s_done, smax_ready, probs_ready = sem("s_done"), sem("smax_ready"), sem("probs_ready")
        pT_done, pT_ready, att_done = sem("pT_done"), sem("pT_ready"), sem("att_done")
        inv_ready, x1_ready, x1b_ready = sem("inv_ready"), sem("x1_ready"), sem("x1b_ready")
        x1T_done, x1T_hi_ready, x1T_lo_ready = sem("x1T_done"), sem("x1T_hi_ready"), sem("x1T_lo_ready")
        kT_done, kmax_ready, kexp_ready = sem("kT_done"), sem("kmax_ready"), sem("kexp_ready")
        kinv_ready, k_done, k_ready = sem("kinv_ready"), sem("k_done"), sem("k_ready")
        qv_done, v_ready, qb_ready, qmax_ready = sem("qv_done"), sem("v_ready"), sem("qb_ready"), sem("qmax_ready")
        qsh_ready, qexp_ready, qsum_ready, qinv_ready, q_ready = (
            sem(n) for n in ("qsh_ready", "qexp_ready", "qsum_ready", "qinv_ready", "q_ready"))
        qT_done, qT_ready, ctx_done, ctx_ready = sem("qT_done"), sem("qT_ready"), sem("ctx_done"), sem("ctx_ready")
        m_done, m_ready, y_done, y_ready = sem("m_done"), sem("m_ready"), sem("y_done"), sem("y_ready")
        stored = sem("stored")

        def active(b):
            return not isinstance(b, int) or 0 <= b < B

        def ready(eng, signal, b):
            eng.wait_ge(signal, b + 1)

        def freed(eng, signal, b):
            if not isinstance(b, int) or b > 0:
                eng.wait_ge(signal, b)

        def pipeline(eng, step):
            for i in range(2):
                step(i)
            with eng.Fori(2, B - 1) as i:
                step(i)
            for i in range(B - 1, B + 2):
                step(i)

        block = ctx.enter_context(nc.Block())

        @block.sync
        def _(sp):
            for b in range(B):
                sp.dma_start(x_all[:, b, :], x_d[b]).then_inc(x_in[b], 16)
            sp.dma_start(w1[:, 0, :], w_qkv[:, 0:C]).then_inc(w1_in, 16)
            sp.dma_start(w1[:, 1, :], w_qkv[:, 2 * C:3 * C]).then_inc(w1_in, 16)
            sp.dma_start(w1[:, 2, :], w_qkv[:, C:2 * C]).then_inc(w1_in, 16)

            with sp.Fori(0, B) as b:
                ready(sp, y_ready, b)
                sp.dma_start(y_d[b], y_all[:, b, :]).then_inc(stored, 16)
            sp.wait_ge(stored, 16 * B)

        @block.gpsimd
        def _(pool):
            pool.memset(ident[:, :], 0.0).then_inc(pool_set, 1)
            pool.memset(group_neg[:, :], -1.0 / GC).then_inc(pool_set, 1)
            pool.memset(head_mask[:, :], 1.0).then_inc(pool_set, 1)
            pool.wait_ge(pool_set, 1)
            pool.affine_select(out=ident[:, :], in_=ident[:, :], compare_op=ALU.not_equal, fill=1.0, base=0,
                               pattern=[[-1, P]], channel_multiplier=1).then_inc(ident_ready, 1)
            pool.memset(neg_half[:, :], -0.5).then_inc(pool_set, 1)
            pool.memset(vals[:, :, C:C + 1], 1.0).then_inc(pool_set, 1)
            n = 5
            for square, side in ((group_neg, GC), (head_mask, HD)):
                v = square[:, :].rearrange("p (g s) -> p g s", s=side)
                pool.wait_ge(pool_set, n)
                pool.affine_select(out=v, in_=v, compare_op=ALU.is_ge, fill=0.0, base=0,
                                   pattern=[[-side, C // side], [0, side]],
                                   channel_multiplier=1).then_inc(pool_set, 1)
                n += 1
                pool.wait_ge(pool_set, n)
                pool.affine_select(out=v, in_=v, compare_op=ALU.is_ge, fill=0.0, base=side - 1,
                                   pattern=[[side, C // side], [0, side]],
                                   channel_multiplier=-1).then_inc(masks_ready, 1)
            pool.wait_ge(var_ready, 1)
            pool.tensor_tensor(rstd[:, :], var_g[:, :], neg_half[:, :], ALU.pow).then_inc(pow_ready, 1)

            def h_lo(b):
                if active(b):
                    ready(pool, h_ready, b)
                    ready(pool, h_hi_ready, b)
                    freed(pool, s_done, b)
                    pool.tensor_tensor(hT_lo[:, :], hT[:, :], hT_hi[:, :].bitcast(F32),
                                       ALU.subtract).then_inc(h_lo_ready, 1)

            def u_lo(b):
                if active(b):
                    ready(pool, u_ready, b)
                    ready(pool, u_hi_ready, b)
                    freed(pool, s_done, b)
                    pool.tensor_tensor(uT_lo[:, :], uT[:, :], uT_hi[:, :].bitcast(F32),
                                       ALU.subtract).then_inc(u_lo_ready, 1)

            def x1_plus_bias(b):
                if active(b):
                    ready(pool, x1_ready, b)
                    if isinstance(b, int) and b == 0:
                        pool.wait_ge(y_bias_ready, 1)
                    pool.tensor_tensor(x1b_all[:, b, :].rearrange("p (j c) -> p j c", j=J),
                                       x1[:, :].rearrange("p (j c) -> p j c", j=J),
                                       y_bias[:, :].unsqueeze(1).to_broadcast([P, J, C]),
                                       ALU.add).then_inc(x1b_ready, 1)

            def q_shift(b):
                if active(b):
                    ready(pool, qmax_ready, b)
                    freed(pool, qexp_ready, b)
                    pool.tensor_tensor(q_sh[:, :].rearrange("p (g d) -> p g d", d=HD),
                                       q_b[:, :, :].rearrange("p j (h d) -> p (j h) d", d=HD),
                                       q_max[:, :].unsqueeze(2).to_broadcast([P, J * HEADS, HD]),
                                       ALU.subtract).then_inc(qsh_ready, 1)

            def q_normal(b):
                if active(b):
                    ready(pool, qinv_ready, b)
                    freed(pool, qT_done, b)
                    pool.tensor_tensor(q_sm[:, :].rearrange("p (g d) -> p g d", d=HD),
                                       q_exp[:, :].rearrange("p (g d) -> p g d", d=HD),
                                       q_inv[:, :].unsqueeze(2).to_broadcast([P, J * HEADS, HD]),
                                       ALU.mult).then_inc(q_ready, 1)

            def step(i):
                u_lo(i)
                x1_plus_bias(i - 1)
                q_shift(i - 1)
                h_lo(i + 1)
                q_normal(i - 1)

            h_lo(0)
            pipeline(pool, step)

        @block.scalar
        def _(act):
            act.dma_start(wq_s[:, :], wq).then_inc(qkw_in, 16)
            act.dma_start(wk_s[:, :], wk).then_inc(qkw_in, 16)
            for r, v in ((GNS, gn_scale), (GNB, gn_bias), (BQ, bq), (BV, bv), (BV1, b_qkv[2 * C:3 * C])):
                act.dma_start(vec_rows[r:r + 1, :], v.rearrange("(a c) -> a c", a=1)).then_inc(vec_in, 16)
            act.dma_start(wv_s[:, :], wv).then_inc(vw_in, 16)
            act.dma_start(wo_s[:, :], wo).then_inc(vw_in, 16)
            act.dma_start(wout_s[:, :], w_out).then_inc(wout_in, 16)
            for t, v in ((gamma_b, gamma.rearrange("a b c d -> (a b c) d")),
                         (bo_b, bo.rearrange("(a c) -> a c", a=1)),
                         (bq1_b, b_qkv[0:C].rearrange("(a c) -> a c", a=1)),
                         (bout_b, b_out.rearrange("(a c) -> a c", a=1)),
                         (beta_b, beta.rearrange("a b c d -> (a b c) d"))):
                act.dma_start(t[:, :], v.to_broadcast([P, C])).then_inc(rows_in, 16)

            for b in range(B):
                act.wait_ge(xT_done, b + 1)
                act.activation(xT_all[:, b, :], xT_ps[b % 4], ACT.Copy).then_inc(xT_copied, 1)
            act.wait_ge(rows_in, 16 * 5)
            act.activation(sig_e[:, :], gamma_b[:, :], ACT.Exp, scale=-1.0).then_inc(sig_exp, 1)

            def u_copy(b):
                if active(b):
                    ready(act, u_done, b)
                    freed(act, s_done, b)
                    act.activation(uT_hi[:, :], u_ps, ACT.Identity, bias=a_bias[:, :]).then_inc(u_hi_ready, 1)
                    freed(act, u_lo_ready, b)
                    act.activation(uT[:, :], u_ps, ACT.Identity, bias=a_bias[:, :]).then_inc(u_ready, 1)

            def s_exp(b):
                if active(b):
                    ready(act, smax_ready, b)
                    freed(act, pT_done, b)
                    for j in range(J):
                        e = act.activation(probs[:, j, :], s_ps[:, j, :], ACT.Exp, bias=neg_smax[:, j:j + 1])
                    e.then_inc(probs_ready, 1)

            def pT_copy(b):
                if active(b):
                    ready(act, pT_done, b)
                    freed(act, att_done, b)
                    act.activation(probsT[:, :, :], s_ps, ACT.Copy).then_inc(pT_ready, 1)

            def x1T_copy(b):
                if active(b):
                    ready(act, x1T_done, b)
                    freed(act, qv_done, b)
                    act.activation(x1T_hi[:, :], x1T_ps, ACT.Copy).then_inc(x1T_hi_ready, 1)

            def k_exp_t(b):
                if active(b):
                    ready(act, kmax_ready, b)
                    freed(act, k_done, b)
                    freed(act, kinv_ready, b)
                    act.activation(kT_exp[:, :], kT_ps, ACT.Exp, bias=neg_kmax[:, :],
                                   accum_out=k_sum[:, :]).then_inc(kexp_ready, 1)

            def v_copy(b):
                if active(b):
                    ready(act, qb_ready, b)
                    freed(act, ctx_done, b)
                    act.activation(v1[:, :, :], qv_ps[:, :, 1, :], ACT.Copy).then_inc(v_ready, 1)

            def k_copy(b):
                if active(b):
                    ready(act, k_done, b)
                    freed(act, ctx_done, b)
                    act.activation(k_exp[:, :], k_ps, ACT.Copy).then_inc(k_ready, 1)

            def q_exp_n(b):
                if active(b):
                    ready(act, qsh_ready, b)
                    freed(act, q_ready, b)
                    act.activation(q_exp[:, :], q_sh[:, :], ACT.Exp).then_inc(qexp_ready, 1)

            def m_copy(b):
                if active(b):
                    ready(act, m_done, b)
                    ready(act, kinv_ready, b)
                    freed(act, y_done, b)
                    act.activation(m_s[:, :], m_ps, ACT.Copy, scale=k_inv[:, :]).then_inc(m_ready, 1)

            def qT_copy(b):
                if active(b):
                    ready(act, qT_done, b)
                    freed(act, y_done, b)
                    act.activation(qT[:, :], qT_ps, ACT.Copy).then_inc(qT_ready, 1)

            def step(i):
                qT_copy(i - 2)
                u_copy(i)
                x1T_copy(i - 1)
                k_exp_t(i - 1)
                s_exp(i)
                q_exp_n(i - 1)
                v_copy(i - 1)
                k_copy(i - 1)
                pT_copy(i)
                m_copy(i - 1)

            pipeline(act, step)

        @block.vector
        def _(dve):
            done = [0]

            def own(ins):
                done[0] += 1
                ins.then_inc(dve_set, 1)
                dve.wait_ge(dve_set, done[0])

            for b in range(B):
                dve.wait_ge(xT_copied, b + 1)
                dve.bn_stats(stats[:, b, :], xT_all[:, b, :]).then_inc(stats_done, 1)
                if b == 1:
                    dve.wait_ge(wT_done, 1)
                    dve.tensor_copy(vec[:, :], wT_ps[:, 3 * C:3 * C + NVEC]).then_inc(wT_copied, 1)
                    dve.tensor_copy(wqT[:, :], wT_ps[:, 0:C]).then_inc(wT_copied, 1)
                    dve.tensor_copy(wkT[:, :], wT_ps[:, C:2 * C]).then_inc(wT_copied, 1)
                    dve.tensor_copy(wvT[:, :], wT_ps[:, 2 * C:3 * C]).then_inc(wT_copied, 1)
                    dve.wait_ge(wT_copied, 4)
                    dve.wait_ge(ident_ready, 1)
                    dve.tensor_copy(bvb[:, :], vec[:, BV:BV + 1].to_broadcast([P, C])).then_inc(wT_copied, 1)
                    dve.tensor_copy(bv1b[:, :], vec[:, BV1:BV1 + 1].to_broadcast([P, C])).then_inc(wT_copied, 1)
            dve.wait_ge(stats_done, B)
            for b in range(B):
                dve.bn_aggr(mv[:, b, :], stats[:, b, :]).then_inc(mv_ready, 1)
            dve.wait_ge(fold_done, 1)
            own(dve.tensor_scalar(a_f[:, :], fold_ps[:, 0:C], SCALE, None, ALU.mult))
            own(dve.tensor_copy(a_hi[:, :], a_f[:, :]))
            dve.tensor_tensor(a_lo[:, :], a_f[:, :], a_hi[:, :].bitcast(F32), ALU.subtract).then_inc(fold_ready, 1)
            dve.tensor_scalar(a_bias[:, :], fold_ps[:, C:C + 1], SCALE, None, ALU.mult).then_inc(fold_ready, 1)
            dve.tensor_copy(wvo[:, :], fold_ps[:, 2 * C:3 * C]).then_inc(fold_ready, 1)
            dve.wait_ge(rows_in, 16 * 5)
            dve.tensor_tensor(val_bias[:, :], fold_ps[:, 3 * C:4 * C], bo_b[:, :], ALU.add).then_inc(fold_ready, 1)
            dve.wait_ge(mean_done, 1)
            own(dve.tensor_copy(neg_mean[:, :], stat_ps[:, 0:B]))
            own(dve.tensor_tensor(dev[:, :], mv[:, :, 0], neg_mean[:, :], ALU.add))
            own(dve.tensor_tensor(dev2[:, :], dev[:, :], dev[:, :], ALU.mult))
            dve.tensor_tensor(var_t[:, :], dev2[:, :], mv[:, :, 1], ALU.add).then_inc(dev_ready, 1)
            dve.wait_ge(var_done, 1)
            dve.tensor_scalar(var_g[:, :], stat_ps[:, B:2 * B], -1.0, EPS, ALU.mult, ALU.add).then_inc(var_ready, 1)
            dve.wait_ge(pow_ready, 1)
            own(dve.tensor_scalar(gn_a[:, :], rstd[:, :], vec[:, GNS:GNS + 1], None, ALU.mult))
            own(dve.tensor_tensor(gn_ba[:, :], neg_mean[:, :], gn_a[:, :], ALU.mult))
            own(dve.tensor_scalar(gn_b[:, :], gn_ba[:, :], vec[:, GNB:GNB + 1], None, ALU.add))

            def h_norm(b):
                if active(b):
                    freed(dve, val_done, b)
                    freed(dve, h_lo_ready, b)
                    dve.tensor_scalar(hT[:, :], xT_all[:, b, :], gn_a[:, bass.ds(b, 1)], gn_b[:, bass.ds(b, 1)],
                                      ALU.mult, ALU.add).then_inc(h_ready, 1)
                    ready(dve, h_ready, b)
                    freed(dve, s_done, b)
                    dve.tensor_copy(hT_hi[:, :], hT[:, :]).then_inc(h_hi_ready, 1)

            def val_copy(b):
                if active(b):
                    ready(dve, val_done, b)
                    freed(dve, att_done, b)
                    dve.tensor_tensor(vals[:, :, 0:C], val_ps, val_bias[:, :].unsqueeze(1).to_broadcast([P, J, C]),
                                      ALU.add).then_inc(val_ready, 1)

            def s_max(b):
                if active(b):
                    ready(dve, s_done, b)
                    freed(dve, probs_ready, b)
                    dve.tensor_reduce(neg_smax[:, :], s_ps, AX_X, ALU.max, negate=True).then_inc(smax_ready, 1)

            def x1_rows(b):
                if active(b):
                    ready(dve, att_done, b)
                    dve.reciprocal(inv_sum[:, :], att_ps[:, :, C]).then_inc(inv_ready, 1)
                    ready(dve, inv_ready, b)
                    freed(dve, x1T_done, b)
                    freed(dve, x1b_ready, b)
                    for j in range(J):
                        r = dve.scalar_tensor_tensor(out=x1[:, j * C:(j + 1) * C], in0=att_ps[:, j, 0:C],
                                                     scalar=inv_sum[:, j:j + 1],
                                                     in1=x_all[:, b, j * C:(j + 1) * C],
                                                     op0=ALU.mult, op1=ALU.add)
                    r.then_inc(x1_ready, 1)

            def x1T_low(b):
                if active(b):
                    ready(dve, x1T_hi_ready, b)
                    freed(dve, qv_done, b)
                    dve.tensor_tensor(x1T_lo[:, :], x1T_ps, x1T_hi[:, :].bitcast(F32),
                                      ALU.subtract).then_inc(x1T_lo_ready, 1)

            def k_max(b):
                if active(b):
                    ready(dve, kT_done, b)
                    freed(dve, kexp_ready, b)
                    dve.tensor_reduce(neg_kmax[:, :], kT_ps, AX_X, ALU.max, negate=True).then_inc(kmax_ready, 1)

            def k_recip(b):
                if active(b):
                    ready(dve, kexp_ready, b)
                    freed(dve, m_ready, b)
                    dve.reciprocal(k_inv[:, :], k_sum[:, :]).then_inc(kinv_ready, 1)

            def q_bias(b):
                if active(b):
                    ready(dve, qv_done, b)
                    freed(dve, qsh_ready, b)
                    dve.tensor_tensor(q_b[:, :, :], qv_ps[:, :, 0, :],
                                      bq1_b[:, :].unsqueeze(1).to_broadcast([P, J, C]), ALU.add).then_inc(qb_ready, 1)

            def q_maxima(b):
                if active(b):
                    ready(dve, qb_ready, b)
                    dve.tensor_reduce(q_max[:, :], q_b[:, :, :].rearrange("p j (h d) -> p (j h) d", d=HD),
                                      AX_X, ALU.max).then_inc(qmax_ready, 1)

            def q_sums(b):
                if active(b):
                    ready(dve, qexp_ready, b)
                    dve.tensor_reduce(q_sum[:, :], q_exp[:, :].rearrange("p (g d) -> p g d", d=HD),
                                      AX_X, ALU.add).then_inc(qsum_ready, 1)
                    ready(dve, qsum_ready, b)
                    freed(dve, q_ready, b)
                    dve.reciprocal(q_inv[:, :], q_sum[:, :]).then_inc(qinv_ready, 1)

            def ctx_mask(b):
                if active(b):
                    ready(dve, ctx_done, b)
                    freed(dve, m_done, b)
                    dve.tensor_tensor(ctxT[:, :], ctx_ps, head_mask[:, :], ALU.mult).then_inc(ctx_ready, 1)

            def y_rows(b):
                if active(b):
                    ready(dve, y_done, b)
                    ready(dve, x1b_ready, b)
                    dve.tensor_tensor(y_all[:, b, :], y_ps, x1b_all[:, b, :], ALU.add).then_inc(y_ready, 1)

            h_norm(0)
            dve.wait_ge(w1_in, 16 * 3)
            own(dve.tensor_copy(w1_hi[:, :, :], w1[:, :, :]))
            dve.tensor_tensor(w1_lo[:, :, :], w1[:, :, :], w1_hi[:, :, :].bitcast(F32),
                              ALU.subtract).then_inc(w1_split, 1)
            dve.wait_ge(sig_exp, 1)
            own(dve.tensor_scalar(sig_d[:, :], sig_e[:, :], 1.0, None, ALU.add))
            own(dve.reciprocal(sig[:, :], sig_d[:, :]))
            dve.wait_ge(wout_in, 16)
            dve.tensor_tensor(wout_sig[:, :], wout_s[:, :], sig[:, :], ALU.mult).then_inc(wout_ready, 1)
            own(dve.tensor_tensor(yb_t[:, :], bout_b[:, :], sig[:, :], ALU.mult))
            own(dve.tensor_tensor(yb_u[:, :], yb_t[:, :], beta_b[:, :], ALU.add))
            dve.wait_ge(bias1_done, 1)
            dve.tensor_tensor(y_bias[:, :], bias1_ps[:, 0:C], yb_u[:, :], ALU.add).then_inc(y_bias_ready, 1)
            dve.wait_ge(masks_ready, 2)

            def step(i):
                val_copy(i)
                x1T_low(i - 1)
                y_rows(i - 2)
                s_max(i)
                k_max(i - 1)
                q_bias(i - 1)
                q_maxima(i - 1)
                k_recip(i - 1)
                ctx_mask(i - 1)
                q_sums(i - 1)
                h_norm(i + 1)
                x1_rows(i)

            pipeline(dve, step)

        @block.tensor
        def _(pe):
            pe.wait_ge(ident_ready, 1)

            def x_transposes(b):
                pe.wait_ge(x_in[b], 16)
                if b >= 4:
                    pe.wait_ge(xT_copied, b - 3)
                for j in range(J):
                    t = pe.transpose(xT_ps[b % 4][:, j * P:(j + 1) * P], x_all[:, b, j * C:(j + 1) * C], ident[:, :])
                t.then_inc(xT_done, 1)

            x_transposes(0)
            x_transposes(1)
            pe.wait_ge(qkw_in, 32)
            pe.wait_ge(vw_in, 32)
            pe.wait_ge(vec_in, 16 * NVEC)
            pe.transpose(wT_ps[:, 3 * C:3 * C + NVEC], vec_rows[:, :], ident[0:NVEC, 0:NVEC])
            pe.transpose(wT_ps[:, 0:C], wq_s[:, :], ident[:, :])
            pe.transpose(wT_ps[:, C:2 * C], wk_s[:, :], ident[:, :])
            pe.transpose(wT_ps[:, 2 * C:3 * C], wv_s[:, :], ident[:, :]).then_inc(wT_done, 1)
            x_transposes(2)
            x_transposes(3)
            pe.wait_ge(wT_copied, 6)
            pe.matmul(fold_ps[:, 0:C], wqT[:, :], wkT[:, :], start=True, stop=True)
            pe.matmul(fold_ps[:, C:C + 1], wkT[:, :], vec[:, BQ:BQ + 1], start=True, stop=True)
            pe.matmul(fold_ps[:, 2 * C:3 * C], wvT[:, :], wo_s[:, :], start=True, stop=True)
            pe.matmul(fold_ps[:, 3 * C:4 * C], bvb[:, :], wo_s[:, :], start=True, stop=True).then_inc(fold_done, 1)
            for b in range(4, B):
                x_transposes(b)
            pe.wait_ge(masks_ready, 1)
            pe.wait_ge(mv_ready, B)
            pe.matmul(stat_ps[:, 0:B], group_neg[:, :], mv[:, :, 0], start=True, stop=True).then_inc(mean_done, 1)
            pe.wait_ge(dev_ready, 1)
            pe.matmul(stat_ps[:, B:2 * B], group_neg[:, :], var_t[:, :], start=True, stop=True).then_inc(var_done, 1)

            def split_product(out_ps, w_hi, w_lo, m_hi, m_lo, lo_signal=None, b=None):
                pe.matmul(out_ps, w_hi, m_hi, start=True, stop=False)
                pe.matmul(out_ps, w_hi, m_lo, start=False, stop=False)
                return pe.matmul(out_ps, w_lo, m_hi, start=False, stop=True)

            def u_product(b):
                if active(b):
                    ready(pe, h_hi_ready, b)
                    ready(pe, h_lo_ready, b)
                    if isinstance(b, int) and b == 0:
                        pe.wait_ge(fold_ready, 4)
                    freed(pe, x1T_lo_ready, b - 1)
                    split_product(u_ps, a_hi[:, :], a_lo[:, :], hT_hi[:, :], hT_lo[:, :]).then_inc(u_done, 1)

            def val_product(b):
                if active(b):
                    ready(pe, h_ready, b)
                    freed(pe, val_ready, b)
                    for j in range(J):
                        m = pe.matmul(val_ps[:, j, :], hT[:, j * P:(j + 1) * P], wvo[:, :], start=True, stop=True)
                    m.then_inc(val_done, 1)

            def s_product(b):
                if active(b):
                    ready(pe, u_hi_ready, b)
                    ready(pe, u_lo_ready, b)
                    freed(pe, pT_ready, b)
                    for j in range(J):
                        rows = slice(j * P, (j + 1) * P)
                        m = split_product(s_ps[:, j, :], uT_hi[:, rows], uT_lo[:, rows], hT_hi[:, :], hT_lo[:, :])
                    m.then_inc(s_done, 1)

            def p_transposes(b):
                if active(b):
                    ready(pe, probs_ready, b)
                    for k in range(J):
                        for j in range(J):
                            t = pe.transpose(s_ps[:, k, j * P:(j + 1) * P], probs[:, j, k * P:(k + 1) * P], ident[:, :])
                    t.then_inc(pT_done, 1)

            def att_product(b):
                if active(b):
                    ready(pe, pT_ready, b)
                    ready(pe, val_ready, b)
                    freed(pe, x1_ready, b)
                    for j in range(J):
                        for k in range(J):
                            m = pe.matmul(att_ps[:, j, :], probsT[:, k, j * P:(j + 1) * P], vals[:, k, :],
                                          start=(k == 0), stop=(k == J - 1))
                    m.then_inc(att_done, 1)

            def x1_transposes(b):
                if active(b):
                    ready(pe, x1_ready, b)
                    if not isinstance(b, int) or b + 1 < B:
                        ready(pe, u_ready, b + 1)
                    for j in range(J):
                        t = pe.transpose(x1T_ps[:, j * P:(j + 1) * P], x1[:, j * C:(j + 1) * C], ident[:, :])
                    t.then_inc(x1T_done, 1)

            def kT_product(b):
                if active(b):
                    ready(pe, x1T_hi_ready, b)
                    ready(pe, x1T_lo_ready, b)
                    if isinstance(b, int) and b == 0:
                        pe.wait_ge(w1_split, 1)
                        pe.wait_ge(y_bias_ready, 1)
                    freed(pe, k_ready, b)
                    split_product(kT_ps, w1_hi[:, 2, :], w1_lo[:, 2, :], x1T_hi[:, :], x1T_lo[:, :]).then_inc(kT_done, 1)

            def qv_product(b):
                if active(b):
                    freed(pe, v_ready, b)
                    freed(pe, qb_ready, b)
                    for j in range(J):
                        rows = slice(j * P, (j + 1) * P)
                        m = split_product(qv_ps[:, j, :, :], x1T_hi[:, rows], x1T_lo[:, rows],
                                          w1_hi[:, 0:2, :], w1_lo[:, 0:2, :])
                    m.then_inc(qv_done, 1)

            def k_transposes(b):
                if active(b):
                    ready(pe, kexp_ready, b)
                    for j in range(J):
                        t = pe.transpose(k_ps[:, j * P:(j + 1) * P], kT_exp[:, j * P:(j + 1) * P], ident[:, :])
                    t.then_inc(k_done, 1)

            def ctx_product(b):
                if active(b):
                    ready(pe, k_ready, b)
                    ready(pe, v_ready, b)
                    freed(pe, y_ready, b)
                    for j in range(J):
                        m = pe.matmul(ctx_ps, v1[:, j, :], k_exp[:, j * C:(j + 1) * C],
                                      start=(j == 0), stop=(j == J - 1))
                    m.then_inc(ctx_done, 1)

            def m_product(b):
                if active(b):
                    ready(pe, ctx_ready, b)
                    pe.matmul(m_ps, ctxT[:, :], wout_sig[:, :], start=True, stop=True).then_inc(m_done, 1)

            def q_transposes(b):
                if active(b):
                    ready(pe, q_ready, b)
                    freed(pe, qT_ready, b)
                    for j in range(J):
                        t = pe.transpose(qT_ps[:, j * P:(j + 1) * P], q_sm[:, j * C:(j + 1) * C], ident[:, :])
                    t.then_inc(qT_done, 1)

            def y_product(b):
                if active(b):
                    ready(pe, qT_ready, b)
                    ready(pe, m_ready, b)
                    for j in range(J):
                        m = pe.matmul(y_ps[:, j * C:(j + 1) * C], qT[:, j * P:(j + 1) * P], m_s[:, :],
                                      start=True, stop=True)
                    m.then_inc(y_done, 1)

            def bias1_product():
                pe.wait_ge(wout_ready, 1)
                pe.matmul(bias1_ps[:, 0:C], bv1b[:, :], wout_sig[:, :], start=True, stop=True).then_inc(bias1_done, 1)

            def step(i):
                u_product(i)
                val_product(i)
                q_transposes(i - 2)
                x1_transposes(i - 1)
                y_product(i - 2)
                s_product(i)
                if isinstance(i, int) and i == 0:
                    bias1_product()
                kT_product(i - 1)
                qv_product(i - 1)
                k_transposes(i - 1)
                p_transposes(i)
                ctx_product(i - 1)
                m_product(i - 1)
                att_product(i)

            pipeline(pe, step)


_INS = ["x", "L0_conv_gn_scale", "L0_conv_gn_bias", "L0_conv_wq", "L0_conv_bq", "L0_conv_wk", "L0_conv_bk",
        "L0_conv_wv", "L0_conv_bv", "L0_conv_wo", "L0_conv_bo", "L1_conv_w_qkv", "L1_conv_b_qkv", "L1_conv_w_out",
        "L1_conv_b_out", "L1_conv_gamma", "L1_conv_beta"]


def kernel(**inputs):
    import numpy as np
    import concourse.bacc as bacc
    from concourse.bass_utils import run_bass_kernel_spmd

    nc = bacc.Bacc("TRN2", target_bir_lowering=False, num_devices=1)
    arrays, args = {}, []
    for name in _INS:
        a = np.ascontiguousarray(inputs[name])
        arrays[f"in_{name}"] = a
        args.append(nc.dram_tensor(f"in_{name}", a.shape, mybir.dt.from_np(a.dtype), kind="ExternalInput").ap())
    y = nc.dram_tensor("out_y", inputs["x"].shape, F32, kind="ExternalOutput").ap()
    build(nc, *args, y)
    r = run_bass_kernel_spmd(nc, [arrays], core_ids=[0])
    return r.results[0]["out_y"]
```

```python
from contextlib import ExitStack

import concourse.bass as bass
from concourse import mybir

F32 = mybir.dt.float32
F32R = mybir.dt.float32r
ALU = mybir.AluOpType
ACT = mybir.ActivationFunctionType
AX_X = mybir.AxisListType.X

GROUPS = 32
HEADS = 8
EPS = 1e-05


def build(nc, x, gn_scale, gn_bias, wq, bq, wk, bk, wv, bv, wo, bo, w_qkv, b_qkv, w_out, b_out, gamma, beta, out):
    B, H, W, C = x.shape
    L = H * W
    P = 128
    J = L // P
    HD = C // HEADS
    GC = C // GROUPS
    SCALE = float(C) ** -0.5
    X_LOADS = [(0, 2), (2, 4), (4, 6), (6, 8)]
    STAT_SETS = [(0, 2), (2, 8)]
    assert C == P and J == 2 and B == 8

    x_d = x.rearrange("b h w c -> b (h w) c").rearrange("b (p j) c -> b p (j c)", j=J)
    y_d = out.rearrange("b h w c -> b (h w) c").rearrange("b (p j) c -> b p (j c)", j=J)

    with ExitStack() as ctx:
        def sb(name, shape, dt=F32):
            return ctx.enter_context(nc.sbuf_tensor(name, shape, dt))

        def ps(name, shape):
            return ctx.enter_context(nc.psum_tensor(name, shape, F32))

        def sem(name):
            return ctx.enter_context(nc.semaphore(name))

        ident = sb("ident", [P, P])
        group_neg = sb("group_neg", [P, P])
        head_mask = sb("head_mask", [P, P])
        wq_s, wk_s, wv_s, wo_s = (sb(n, [P, C]) for n in ("wq_s", "wk_s", "wv_s", "wo_s"))
        w1 = sb("w1", [P, 3, C])
        w1_hi = sb("w1_hi", [P, 3, C], F32R)
        w1_lo = sb("w1_lo", [P, 3, C], F32R)
        wout_s = sb("wout_s", [P, C])
        wout_sig = sb("wout_sig", [P, C])
        VECS = 11
        GNS, GNB, BQ, BV, BO, BQ1, BK1, BV1, BOUT, GAMMA, BETA = range(VECS)
        vec_rows = sb("vec_rows", [VECS, C])
        turned = sb("turned", [P, 3 * C])
        wqT, wkT, wvT = (turned[:, n * C:(n + 1) * C] for n in range(3))
        vec = sb("vec", [P, VECS])
        ones = sb("ones", [P, P])
        bo_diag, bq1_diag, sig_diag, yb_diag = (sb(n, [P, C]) for n in ("bo_diag", "bq1_diag", "sig_diag", "yb_diag"))
        bq1_b = sb("bq1_b", [P, C])
        a_hi = sb("a_hi", [P, C], F32R)
        a_lo = sb("a_lo", [P, C], F32R)
        a_bias = sb("a_bias", [P, 1])
        wvo = sb("wvo", [P, C])
        bvb = sb("bvb", [P, C])
        bv1b = sb("bv1b", [P, C])
        val_bias = sb("val_bias", [P, C])
        y_bias = sb("y_bias", [P, C])
        sig_e, sig_d, sig, yb_t, yb_u = (sb(n, [P, 1]) for n in ("sig_e", "sig_d", "sig", "yb_t", "yb_u"))
        neg_half = sb("neg_half", [P, B])
        warm = sb("warm", [P, 1])

        x_all = sb("x_all", [P, B, J * C])
        xT_all = sb("xT_all", [P, B, L])
        x1b_all = sb("x1b_all", [P, B, J * C])
        y_all = sb("y_all", [P, B, J * C])
        stats = sb("stats", [P, B, 6])
        mv = sb("mv", [P, B, 2])
        dev = sb("dev", [P, B])
        dev2 = sb("dev2", [P, B])
        var_t = sb("var_t", [P, B])
        var_g = sb("var_g", [P, B])
        rstd = sb("rstd", [P, B])
        gn_a = sb("gn_a", [P, B])
        neg_mean = sb("neg_mean", [P, B])
        gn_ba = sb("gn_ba", [P, B])
        gn_b = sb("gn_b", [P, B])

        hT = sb("hT", [P, L])
        hT_hi = sb("hT_hi", [P, L], F32R)
        hT_lo = sb("hT_lo", [P, L], F32R)
        uT_hi = sb("uT_hi", [P, L], F32R)
        uT_lo = sb("uT_lo", [P, L], F32R)
        vals = sb("vals", [P, J, C + 1])
        neg_smax = sb("neg_smax", [P, J])
        probs = sb("probs", [P, J, L])
        probsT = sb("probsT", [P, J, L])
        inv_sum = sb("inv_sum", [P, J])
        x1 = sb("x1", [P, J * C])
        x1T_hi = sb("x1T_hi", [P, L], F32R)
        x1T_lo = sb("x1T_lo", [P, L], F32R)
        neg_kmax = sb("neg_kmax", [P, 1])
        kT_exp = sb("kT_exp", [P, L])
        k_sum = sb("k_sum", [P, 1])
        k_inv = sb("k_inv", [P, 1])
        k_exp = sb("k_exp", [P, J * C])
        v1 = sb("v1", [P, J, C])
        q_b = sb("q_b", [P, J, C])
        q_max = sb("q_max", [P, J * HEADS])
        q_sh = sb("q_sh", [P, J * C])
        q_exp = sb("q_exp", [P, J * C])
        q_sum = sb("q_sum", [P, J * HEADS])
        q_inv = sb("q_inv", [P, J * HEADS])
        q_sm = sb("q_sm", [P, J * C])
        qT = sb("qT", [P, L])
        ctxT = sb("ctxT", [P, C])
        m_s = sb("m_s", [P, C])

        b_u = ps("b_u", [P, 512])
        b_val = ps("b_val", [P, 512])
        b_s = ps("b_s", [P, 512])
        b_att = ps("b_att", [P, 512])
        b_k = ps("b_k", [P, 512])
        b_qv = ps("b_qv", [P, 512])
        b_q = ps("b_q", [P, 512])
        b_y = ps("b_y", [P, 512])
        u_ps = b_u[:, 0:L]
        val_ps = b_val[:, 0:J * C].rearrange("p (j c) -> p j c", j=J)
        s_ps = b_s[:, :].rearrange("p (j l) -> p j l", j=J)
        att_ps = b_att[:, 0:J * (C + 1)].rearrange("p (j c) -> p j c", j=J)
        x1T_ps, kT_ps, k_ps = b_k[:, 0:L], b_k[:, L:2 * L], b_k[:, 0:L]
        qv_ps = b_qv[:, :].rearrange("p (j a c) -> p j a c", j=J, a=2)
        qT_ps = b_q[:, 0:L]
        ctx_ps, m_ps, y_ps = b_y[:, 0:C], b_y[:, C:2 * C], b_y[:, 2 * C:2 * C + J * C]
        XT_BANKS = [b_y, b_q, b_qv, b_k]
        xT_ps = [b[:, 0:L] for b in XT_BANKS]
        wT_ps, vecT_ps, a_ps, fold_ps, stat_ps, rows_ps = b_s, b_att, b_u, b_val, b_s, b_att

        x_in = [sem(f"x_in{n}") for n in range(len(X_LOADS))]
        qk_in, vo_in, w1_in, wout_in, vec_in, gn_in = (
            sem(n) for n in ("qk_in", "vo_in", "w1_in", "wout_in", "vec_in", "gn_in"))
        zero_set, pool_set, ident_ready, group_ready, heads_ready, pow_ready = (
            sem(n) for n in ("zero_set", "pool_set", "ident_ready", "group_ready", "heads_ready", "pow_ready"))
        xT_done, stats_done, xT_copied = sem("xT_done"), sem("stats_done"), sem("xT_copied")
        wT_done, wT_copied, vecT_done, vec_ready = sem("wT_done"), sem("wT_copied"), sem("vecT_done"), sem("vec_ready")
        dve_set, stat_free = sem("dve_set"), sem("stat_free")
        mv_ready, mean_done, dev_ready, var_done, var_ready = (
            sem(n) for n in ("mv_ready", "mean_done", "dev_ready", "var_done", "var_ready"))
        a_done, a_hi_ready, a_lo_ready, diag_ready, fold_done, fold_ready, w1_split = (
            sem(n) for n in ("a_done", "a_hi_ready", "a_lo_ready", "diag_ready", "fold_done", "fold_ready", "w1_split"))
        sig_exp, sig_diag_ready, sig_rows, wout_ready, yb_diag_ready, y_rows_done, rows_ready = (
            sem(n) for n in ("sig_exp", "sig_diag_ready", "sig_rows", "wout_ready", "yb_diag_ready", "y_rows_done",
                             "rows_ready"))
        h_ready, h_hi_ready, h_lo_ready = sem("h_ready"), sem("h_hi_ready"), sem("h_lo_ready")
        u_done, u_hi_ready, u_lo_ready = sem("u_done"), sem("u_hi_ready"), sem("u_lo_ready")
        val_done, val_ready = sem("val_done"), sem("val_ready")
        s_done, smax_ready, probs_ready = sem("s_done"), sem("smax_ready"), sem("probs_ready")
        pT_done, pT_ready, att_done = sem("pT_done"), sem("pT_ready"), sem("att_done")
        inv_ready, x1_ready, x1b_ready = sem("inv_ready"), sem("x1_ready"), sem("x1b_ready")
        x1T_done, x1T_hi_ready, x1T_lo_ready = sem("x1T_done"), sem("x1T_hi_ready"), sem("x1T_lo_ready")
        kT_done, kmax_ready, kexp_ready = sem("kT_done"), sem("kmax_ready"), sem("kexp_ready")
        kinv_ready, k_done, k_ready = sem("kinv_ready"), sem("k_done"), sem("k_ready")
        qv_done, v_ready, qb_ready, qmax_ready = sem("qv_done"), sem("v_ready"), sem("qb_ready"), sem("qmax_ready")
        qsh_ready, qexp_ready, qsum_ready, qinv_ready, q_ready = (
            sem(n) for n in ("qsh_ready", "qexp_ready", "qsum_ready", "qinv_ready", "q_ready"))
        qT_done, qT_ready, ctx_done, ctx_ready = sem("qT_done"), sem("qT_ready"), sem("ctx_done"), sem("ctx_ready")
        m_done, m_ready, y_done, y_ready = sem("m_done"), sem("m_ready"), sem("y_done"), sem("y_ready")
        stored = sem("stored")

        def active(b):
            return not isinstance(b, int) or 0 <= b < B

        def ready(eng, signal, b):
            eng.wait_ge(signal, b + 1)

        def freed(eng, signal, b):
            if not isinstance(b, int) or b > 0:
                eng.wait_ge(signal, b)

        def at(b, n):
            return isinstance(b, int) and b == n

        DEPTH = 3

        def pipeline(eng, step):
            for i in range(DEPTH):
                step(i)
            with eng.Fori(DEPTH, B) as i:
                step(i)
            for i in range(B, B + DEPTH):
                step(i)

        block = ctx.enter_context(nc.Block())

        @block.sync
        def _(sp):
            def load_x(n):
                a, b = X_LOADS[n]
                sp.dma_start(x_all[:, a:b, :], x_d[a:b].rearrange("b p f -> p b f")).then_inc(x_in[n], 16)

            def load_vec(r, v):
                sp.dma_start(vec_rows[r:r + v.shape[0], :], v).then_inc(vec_in, 16)

            load_x(0)
            sp.dma_start(wq_s[:, :], wq).then_inc(qk_in, 16)
            sp.dma_start(wk_s[:, :], wk).then_inc(qk_in, 16)
            load_vec(BO, bo.rearrange("(a c) -> a c", a=1))
            load_x(1)
            sp.dma_start(wv_s[:, :], wv).then_inc(vo_in, 16)
            sp.dma_start(wo_s[:, :], wo).then_inc(vo_in, 16)
            load_x(2)
            load_x(3)
            sp.dma_start(w1[:, :, :], w_qkv.rearrange("k (a c) -> k a c", a=3)).then_inc(w1_in, 16)
            sp.dma_start(wout_s[:, :], w_out).then_inc(wout_in, 16)

            with sp.Fori(0, B) as b:
                ready(sp, y_ready, b)
                sp.dma_start(y_d[b], y_all[:, b, :]).then_inc(stored, 16)
            sp.wait_ge(stored, 16 * B)

        @block.gpsimd
        def _(pool):
            pool.memset(ident[:, :], 0.0).then_inc(zero_set, 1)
            pool.wait_ge(zero_set, 1)
            pool.affine_select(out=ident[:, :], in_=ident[:, :], compare_op=ALU.not_equal, fill=1.0, base=0,
                               pattern=[[-1, P]], channel_multiplier=1).then_inc(ident_ready, 1)
            for r, v in ((GNS, gn_scale), (GNB, gn_bias)):
                pool.dma_start(vec_rows[r:r + 1, :], v.rearrange("(a c) -> a c", a=1)).then_inc(gn_in, 16)
            pool.memset(neg_half[:, :], -0.5)
            pool.memset(ones[:, :], 1.0).then_inc(pool_set, 1)
            pool.memset(vals[:, :, C:C + 1], 1.0)
            pool.memset(group_neg[:, :], -1.0 / GC)
            pool.memset(head_mask[:, :], 1.0).then_inc(pool_set, 1)
            n = 2
            for square, side, signal in ((group_neg, GC, group_ready), (head_mask, HD, heads_ready)):
                v = square[:, :].rearrange("p (g s) -> p g s", s=side)
                pool.wait_ge(pool_set, n)
                pool.affine_select(out=v, in_=v, compare_op=ALU.is_ge, fill=0.0, base=0,
                                   pattern=[[-side, C // side], [0, side]],
                                   channel_multiplier=1).then_inc(pool_set, 1)
                n += 1
                pool.wait_ge(pool_set, n)
                pool.affine_select(out=v, in_=v, compare_op=ALU.is_ge, fill=0.0, base=side - 1,
                                   pattern=[[side, C // side], [0, side]],
                                   channel_multiplier=-1).then_inc(signal, 1)

            def inv_std(n):
                a, b = STAT_SETS[n]
                pool.wait_ge(var_ready, n + 1)
                pool.tensor_tensor(rstd[:, a:b], var_g[:, a:b], neg_half[:, a:b], ALU.pow).then_inc(pow_ready, 1)

            inv_std(0)

            def h_lo(b):
                if active(b):
                    ready(pool, h_ready, b)
                    ready(pool, h_hi_ready, b)
                    freed(pool, s_done, b)
                    pool.tensor_tensor(hT_lo[:, :], hT[:, :], hT_hi[:, :].bitcast(F32),
                                       ALU.subtract).then_inc(h_lo_ready, 1)

            def x1_plus_bias(b):
                if active(b):
                    ready(pool, x1_ready, b)
                    if isinstance(b, int) and b == 0:
                        pool.wait_ge(rows_ready, 1)
                    pool.tensor_tensor(x1b_all[:, b, :].rearrange("p (j c) -> p j c", j=J),
                                       x1[:, :].rearrange("p (j c) -> p j c", j=J),
                                       y_bias[:, :].unsqueeze(1).to_broadcast([P, J, C]),
                                       ALU.add).then_inc(x1b_ready, 1)

            def q_shift(b):
                if active(b):
                    ready(pool, qmax_ready, b)
                    freed(pool, qexp_ready, b)
                    pool.tensor_tensor(q_sh[:, :].rearrange("p (g d) -> p g d", d=HD),
                                       q_b[:, :, :].rearrange("p j (h d) -> p (j h) d", d=HD),
                                       q_max[:, :].unsqueeze(2).to_broadcast([P, J * HEADS, HD]),
                                       ALU.subtract).then_inc(qsh_ready, 1)

            def q_normal(b):
                if active(b):
                    ready(pool, qinv_ready, b)
                    freed(pool, qT_done, b)
                    pool.tensor_tensor(q_sm[:, :].rearrange("p (g d) -> p g d", d=HD),
                                       q_exp[:, :].rearrange("p (g d) -> p g d", d=HD),
                                       q_inv[:, :].unsqueeze(2).to_broadcast([P, J * HEADS, HD]),
                                       ALU.mult).then_inc(q_ready, 1)

            def step(i):
                h_lo(i)
                if at(i, 0):
                    inv_std(1)
                x1_plus_bias(i - 1)
                q_normal(i - 2)
                q_shift(i - 1)

            pipeline(pool, step)

        @block.scalar
        def _(act):
            for r, v in ((BQ, bq.rearrange("(a c) -> a c", a=1)), (BV, bv.rearrange("(a c) -> a c", a=1)),
                         (BQ1, b_qkv.rearrange("(a c) -> a c", a=3)), (BOUT, b_out.rearrange("(a c) -> a c", a=1)),
                         (GAMMA, gamma.rearrange("a b c d -> (a b c) d")),
                         (BETA, beta.rearrange("a b c d -> (a b c) d"))):
                act.dma_start(vec_rows[r:r + v.shape[0], :], v).then_inc(vec_in, 16)
            act.wait_ge(ident_ready, 1)
            act.activation(warm[:, :], ident[:, 0:1], ACT.Exp)

            def xT_copy(b):
                act.wait_ge(stats_done, b + 1)
                act.activation(xT_all[:, b, :], xT_ps[b % 4], ACT.Copy).then_inc(xT_copied, 1)

            act.wait_ge(wT_done, 1)
            act.activation(turned[:, :], wT_ps[:, 0:3 * C], ACT.Copy).then_inc(wT_copied, 1)
            xT_copy(0)
            xT_copy(1)
            act.wait_ge(a_done, 1)
            act.activation(a_hi[:, :], a_ps[:, 0:C], ACT.Copy, scale=SCALE).then_inc(a_hi_ready, 1)
            act.wait_ge(fold_done, 1)
            act.activation(wvo[:, :], fold_ps[:, 0:C], ACT.Copy)
            act.activation(val_bias[:, :], fold_ps[:, C:2 * C], ACT.Copy)
            act.activation(a_bias[:, :], fold_ps[:, 2 * C:2 * C + 1], ACT.Copy, scale=SCALE).then_inc(fold_ready, 1)
            act.wait_ge(vec_ready, 1)
            act.activation(sig_e[:, :], vec[:, GAMMA:GAMMA + 1], ACT.Exp, scale=-1.0).then_inc(sig_exp, 1)
            for b in range(2, B):
                xT_copy(b)

            def u_high(b):
                if active(b):
                    ready(act, u_done, b)
                    if isinstance(b, int) and b == 0:
                        act.wait_ge(fold_ready, 1)
                    freed(act, s_done, b)
                    act.activation(uT_hi[:, :], u_ps, ACT.Identity, bias=a_bias[:, :]).then_inc(u_hi_ready, 1)

            def s_exp(b):
                if active(b):
                    ready(act, smax_ready, b)
                    freed(act, pT_done, b)
                    for j in range(J):
                        e = act.activation(probs[:, j, :], s_ps[:, j, :], ACT.Exp, bias=neg_smax[:, j:j + 1])
                    e.then_inc(probs_ready, 1)

            def pT_copy(b):
                if active(b):
                    ready(act, pT_done, b)
                    freed(act, att_done, b)
                    act.activation(probsT[:, :, :], s_ps, ACT.Copy).then_inc(pT_ready, 1)

            def x1T_high(b):
                if active(b):
                    ready(act, x1T_done, b)
                    freed(act, qv_done, b)
                    act.activation(x1T_hi[:, :], x1T_ps, ACT.Copy).then_inc(x1T_hi_ready, 1)

            def k_exp_t(b):
                if active(b):
                    ready(act, kmax_ready, b)
                    freed(act, k_done, b)
                    freed(act, kinv_ready, b)
                    act.activation(kT_exp[:, :], kT_ps, ACT.Exp, bias=neg_kmax[:, :],
                                   accum_out=k_sum[:, :]).then_inc(kexp_ready, 1)

            def v_copy(b):
                if active(b):
                    ready(act, qb_ready, b)
                    freed(act, ctx_done, b)
                    act.activation(v1[:, :, :], qv_ps[:, :, 1, :], ACT.Copy).then_inc(v_ready, 1)

            def k_copy(b):
                if active(b):
                    ready(act, k_done, b)
                    freed(act, ctx_done, b)
                    act.activation(k_exp[:, :], k_ps, ACT.Copy).then_inc(k_ready, 1)

            def q_exp_n(b):
                if active(b):
                    ready(act, qsh_ready, b)
                    freed(act, q_ready, b)
                    act.activation(q_exp[:, :], q_sh[:, :], ACT.Exp).then_inc(qexp_ready, 1)

            def m_copy(b):
                if active(b):
                    ready(act, m_done, b)
                    ready(act, kinv_ready, b)
                    freed(act, y_done, b)
                    act.activation(m_s[:, :], m_ps, ACT.Copy, scale=k_inv[:, :]).then_inc(m_ready, 1)

            def qT_copy(b):
                if active(b):
                    ready(act, qT_done, b)
                    freed(act, y_done, b)
                    act.activation(qT[:, :], qT_ps, ACT.Copy).then_inc(qT_ready, 1)

            def step(i):
                k_copy(i - 2)
                u_high(i)
                x1T_high(i - 1)
                m_copy(i - 2)
                s_exp(i)
                qT_copy(i - 2)
                k_exp_t(i - 1)
                pT_copy(i)
                v_copy(i - 1)
                q_exp_n(i - 1)

            pipeline(act, step)

        @block.vector
        def _(dve):
            done = [0]

            def own(ins):
                done[0] += 1
                ins.then_inc(dve_set, 1)
                dve.wait_ge(dve_set, done[0])

            def channel_stats(b):
                dve.wait_ge(xT_done, b + 1)
                dve.bn_stats(stats[:, b, :], xT_ps[b % 4]).then_inc(stats_done, 1)

            def set_means(n):
                a, b = STAT_SETS[n]
                dve.wait_ge(stats_done, b)
                for k in range(a, b):
                    dve.bn_aggr(mv[:, k, :], stats[:, k, :]).then_inc(mv_ready, 1)

            def set_deviations(n):
                a, b = STAT_SETS[n]
                dve.wait_ge(mean_done, n + 1)
                own(dve.tensor_tensor(dev[:, a:b], mv[:, a:b, 0], stat_ps[:, a:b], ALU.add))
                own(dve.tensor_tensor(dev2[:, a:b], dev[:, a:b], dev[:, a:b], ALU.mult))
                dve.tensor_tensor(var_t[:, a:b], dev2[:, a:b], mv[:, a:b, 1], ALU.add).then_inc(dev_ready, 1)

            def set_variances(n):
                a, b = STAT_SETS[n]
                dve.wait_ge(var_done, n + 1)
                dve.tensor_scalar(var_g[:, a:b], stat_ps[:, B + a:B + b], -1.0, EPS,
                                  ALU.mult, ALU.add).then_inc(var_ready, 1)
                dve.tensor_copy(neg_mean[:, a:b], stat_ps[:, a:b]).then_inc(stat_free, 1)

            def set_scales(n):
                a, b = STAT_SETS[n]
                dve.wait_ge(pow_ready, n + 1)
                own(dve.tensor_scalar(gn_a[:, a:b], rstd[:, a:b], vec[:, GNS:GNS + 1], None, ALU.mult))
                own(dve.tensor_tensor(gn_ba[:, a:b], neg_mean[:, a:b], gn_a[:, a:b], ALU.mult))
                own(dve.tensor_scalar(gn_b[:, a:b], gn_ba[:, a:b], vec[:, GNB:GNB + 1], None, ALU.add))

            channel_stats(0)
            channel_stats(1)
            set_means(0)
            set_deviations(0)
            dve.wait_ge(vecT_done, 1)
            own(dve.tensor_copy(vec[:, :], vecT_ps[:, 0:VECS]))
            set_variances(0)
            dve.tensor_scalar(bo_diag[:, :], ident[:, :], vec[:, BO:BO + 1], None, ALU.mult)
            dve.tensor_copy(bvb[:, :], vec[:, BV:BV + 1].to_broadcast([P, C])).then_inc(diag_ready, 1)
            dve.tensor_scalar(bq1_diag[:, :], ident[:, :], vec[:, BQ1:BQ1 + 1], None, ALU.mult)
            dve.tensor_copy(bv1b[:, :], vec[:, BV1:BV1 + 1].to_broadcast([P, C])).then_inc(vec_ready, 1)
            dve.wait_ge(a_hi_ready, 1)
            dve.scalar_tensor_tensor(out=a_lo[:, :], in0=a_ps[:, 0:C], scalar=SCALE, in1=a_hi[:, :].bitcast(F32),
                                     op0=ALU.mult, op1=ALU.subtract).then_inc(a_lo_ready, 1)
            for b in range(2, B):
                channel_stats(b)
            set_scales(0)

            def h_norm(b):
                if active(b):
                    freed(dve, val_done, b)
                    freed(dve, h_lo_ready, b)
                    dve.tensor_scalar(hT[:, :], xT_all[:, b, :], gn_a[:, bass.ds(b, 1)], gn_b[:, bass.ds(b, 1)],
                                      ALU.mult, ALU.add).then_inc(h_ready, 1)
                    ready(dve, h_ready, b)
                    freed(dve, s_done, b)
                    dve.tensor_copy(hT_hi[:, :], hT[:, :]).then_inc(h_hi_ready, 1)

            def u_low(b):
                if active(b):
                    ready(dve, u_hi_ready, b)
                    freed(dve, s_done, b)
                    dve.scalar_tensor_tensor(out=uT_lo[:, :], in0=u_ps, scalar=a_bias[:, :],
                                             in1=uT_hi[:, :].bitcast(F32), op0=ALU.add,
                                             op1=ALU.subtract).then_inc(u_lo_ready, 1)

            def val_copy(b):
                if active(b):
                    ready(dve, val_done, b)
                    freed(dve, att_done, b)
                    dve.tensor_tensor(vals[:, :, 0:C], val_ps, val_bias[:, :].unsqueeze(1).to_broadcast([P, J, C]),
                                      ALU.add).then_inc(val_ready, 1)

            def s_max(b):
                if active(b):
                    ready(dve, s_done, b)
                    freed(dve, probs_ready, b)
                    dve.tensor_reduce(neg_smax[:, :], s_ps, AX_X, ALU.max, negate=True).then_inc(smax_ready, 1)

            def x1_rows(b):
                if active(b):
                    ready(dve, att_done, b)
                    dve.reciprocal(inv_sum[:, :], att_ps[:, :, C]).then_inc(inv_ready, 1)
                    ready(dve, inv_ready, b)
                    freed(dve, x1T_done, b)
                    freed(dve, x1b_ready, b)
                    for j in range(J):
                        r = dve.scalar_tensor_tensor(out=x1[:, j * C:(j + 1) * C], in0=att_ps[:, j, 0:C],
                                                     scalar=inv_sum[:, j:j + 1],
                                                     in1=x_all[:, b, j * C:(j + 1) * C],
                                                     op0=ALU.mult, op1=ALU.add)
                    r.then_inc(x1_ready, 1)

            def x1T_low(b):
                if active(b):
                    ready(dve, x1T_hi_ready, b)
                    freed(dve, qv_done, b)
                    dve.tensor_tensor(x1T_lo[:, :], x1T_ps, x1T_hi[:, :].bitcast(F32),
                                      ALU.subtract).then_inc(x1T_lo_ready, 1)

            def k_max(b):
                if active(b):
                    ready(dve, kT_done, b)
                    freed(dve, kexp_ready, b)
                    dve.tensor_reduce(neg_kmax[:, :], kT_ps, AX_X, ALU.max, negate=True).then_inc(kmax_ready, 1)

            def k_recip(b):
                if active(b):
                    ready(dve, kexp_ready, b)
                    freed(dve, m_ready, b)
                    dve.reciprocal(k_inv[:, :], k_sum[:, :]).then_inc(kinv_ready, 1)

            def q_bias(b):
                if active(b):
                    ready(dve, qv_done, b)
                    freed(dve, qsh_ready, b)
                    dve.tensor_tensor(q_b[:, :, :], qv_ps[:, :, 0, :],
                                      bq1_b[:, :].unsqueeze(1).to_broadcast([P, J, C]), ALU.add).then_inc(qb_ready, 1)

            def q_maxima(b):
                if active(b):
                    ready(dve, qb_ready, b)
                    dve.tensor_reduce(q_max[:, :], q_b[:, :, :].rearrange("p j (h d) -> p (j h) d", d=HD),
                                      AX_X, ALU.max).then_inc(qmax_ready, 1)

            def q_sums(b):
                if active(b):
                    ready(dve, qexp_ready, b)
                    dve.tensor_reduce(q_sum[:, :], q_exp[:, :].rearrange("p (g d) -> p g d", d=HD),
                                      AX_X, ALU.add).then_inc(qsum_ready, 1)
                    ready(dve, qsum_ready, b)
                    freed(dve, q_ready, b)
                    dve.reciprocal(q_inv[:, :], q_sum[:, :]).then_inc(qinv_ready, 1)

            def ctx_mask(b):
                if active(b):
                    ready(dve, ctx_done, b)
                    freed(dve, m_done, b)
                    dve.tensor_tensor(ctxT[:, :], ctx_ps, head_mask[:, :], ALU.mult).then_inc(ctx_ready, 1)

            def y_rows(b):
                if active(b):
                    ready(dve, y_done, b)
                    ready(dve, x1b_ready, b)
                    dve.tensor_tensor(y_all[:, b, :], y_ps, x1b_all[:, b, :], ALU.add).then_inc(y_ready, 1)

            def set_w1():
                dve.wait_ge(w1_in, 16)
                own(dve.tensor_copy(w1_hi[:, :, :], w1[:, :, :]))
                dve.tensor_tensor(w1_lo[:, :, :], w1[:, :, :], w1_hi[:, :, :].bitcast(F32),
                                  ALU.subtract).then_inc(w1_split, 1)

            def set_sigmoid():
                dve.wait_ge(sig_exp, 1)
                own(dve.tensor_scalar(sig_d[:, :], sig_e[:, :], 1.0, None, ALU.add))
                own(dve.reciprocal(sig[:, :], sig_d[:, :]))
                dve.tensor_scalar(sig_diag[:, :], ident[:, :], sig[:, :], None, ALU.mult).then_inc(sig_diag_ready, 1)
                own(dve.tensor_tensor(yb_t[:, :], vec[:, BOUT:BOUT + 1], sig[:, :], ALU.mult))
                own(dve.tensor_tensor(yb_u[:, :], yb_t[:, :], vec[:, BETA:BETA + 1], ALU.add))
                dve.tensor_scalar(yb_diag[:, :], ident[:, :], yb_u[:, :], None, ALU.mult).then_inc(yb_diag_ready, 1)

            def set_wout():
                dve.wait_ge(wout_in, 16)
                dve.wait_ge(sig_rows, 1)
                dve.tensor_copy(bq1_b[:, :], rows_ps[:, C:2 * C])
                dve.tensor_tensor(wout_sig[:, :], wout_s[:, :], rows_ps[:, 0:C], ALU.mult).then_inc(wout_ready, 1)

            def set_y_bias():
                dve.wait_ge(y_rows_done, 1)
                dve.tensor_copy(y_bias[:, :], rows_ps[:, 2 * C:3 * C]).then_inc(rows_ready, 1)

            def step(i):
                h_norm(i)
                if at(i, 0):
                    set_means(1)
                if at(i, 0):
                    set_deviations(1)
                y_rows(i - 3)
                q_sums(i - 2)
                x1_rows(i - 1)
                u_low(i)
                if at(i, 0):
                    set_variances(1)
                val_copy(i)
                if at(i, 0):
                    set_w1()
                if at(i, 0):
                    set_scales(1)
                k_recip(i - 2)
                ctx_mask(i - 2)
                x1T_low(i - 1)
                s_max(i)
                if at(i, 0):
                    set_sigmoid()
                if at(i, 0):
                    set_wout()
                if at(i, 0):
                    set_y_bias()
                k_max(i - 1)
                q_bias(i - 1)
                q_maxima(i - 1)

            pipeline(dve, step)

        @block.tensor
        def _(pe):
            def x_transposes(b):
                for n, (a, z) in enumerate(X_LOADS):
                    if b == a:
                        pe.wait_ge(x_in[n], 16)
                if b >= 4:
                    pe.wait_ge(xT_copied, b - 3)
                for j in range(J):
                    t = pe.transpose(xT_ps[b % 4][:, j * P:(j + 1) * P], x_all[:, b, j * C:(j + 1) * C], ident[:, :])
                t.then_inc(xT_done, 1)

            def means(n):
                a, b = STAT_SETS[n]
                pe.wait_ge(mv_ready, b)
                if n:
                    pe.wait_ge(stat_free, n)
                pe.matmul(stat_ps[:, a:b], group_neg[:, :], mv[:, a:b, 0], start=True, stop=True).then_inc(mean_done, 1)

            def variances(n):
                a, b = STAT_SETS[n]
                pe.wait_ge(dev_ready, n + 1)
                pe.matmul(stat_ps[:, B + a:B + b], group_neg[:, :], var_t[:, a:b],
                          start=True, stop=True).then_inc(var_done, 1)

            pe.wait_ge(ident_ready, 1)
            x_transposes(0)
            x_transposes(1)
            pe.wait_ge(qk_in, 32)
            pe.wait_ge(vo_in, 32)
            for n, w in enumerate((wq_s, wk_s, wv_s)):
                t = pe.transpose(wT_ps[:, n * C:(n + 1) * C], w[:, :], ident[:, :])
            t.then_inc(wT_done, 1)
            pe.wait_ge(wT_copied, 1)
            pe.matmul(a_ps[:, 0:C], wqT, wkT, start=True, stop=True).then_inc(a_done, 1)
            pe.wait_ge(group_ready, 1)
            means(0)
            pe.wait_ge(vec_in, 16 * 7)
            pe.wait_ge(gn_in, 32)
            pe.transpose(vecT_ps[:, 0:VECS], vec_rows[:, :], ident[0:VECS, 0:VECS]).then_inc(vecT_done, 1)
            variances(0)
            pe.wait_ge(diag_ready, 1)
            pe.wait_ge(pool_set, 1)
            pe.matmul(fold_ps[:, 0:C], wvT, wo_s[:, :], start=True, stop=True)
            pe.matmul(fold_ps[:, C:2 * C], bvb[:, :], wo_s[:, :], start=True, stop=False)
            pe.matmul(fold_ps[:, C:2 * C], ones[:, :], bo_diag[:, :], start=False, stop=True)
            pe.matmul(fold_ps[:, 2 * C:2 * C + 1], wkT, vec[:, BQ:BQ + 1], start=True, stop=True).then_inc(fold_done, 1)
            for b in range(2, B):
                x_transposes(b)

            means(1)

            def sigmoid_rows():
                pe.wait_ge(sig_diag_ready, 1)
                pe.matmul(rows_ps[:, 0:C], ones[:, :], sig_diag[:, :], start=True, stop=True)
                pe.matmul(rows_ps[:, C:2 * C], ones[:, :], bq1_diag[:, :], start=True, stop=True).then_inc(sig_rows, 1)

            def y_bias_rows():
                pe.wait_ge(wout_ready, 1)
                pe.wait_ge(yb_diag_ready, 1)
                pe.matmul(rows_ps[:, 2 * C:3 * C], bv1b[:, :], wout_sig[:, :], start=True, stop=False)
                pe.matmul(rows_ps[:, 2 * C:3 * C], ones[:, :], yb_diag[:, :], start=False, stop=True).then_inc(y_rows_done, 1)

            def split_product(out_ps, w_hi, w_lo, m_hi, m_lo, lo_signal=None, b=None):
                pe.matmul(out_ps, w_hi, m_hi, start=True, stop=False)
                pe.matmul(out_ps, w_hi, m_lo, start=False, stop=False)
                return pe.matmul(out_ps, w_lo, m_hi, start=False, stop=True)

            def u_product(b):
                if active(b):
                    ready(pe, h_hi_ready, b)
                    ready(pe, h_lo_ready, b)
                    if isinstance(b, int) and b == 0:
                        pe.wait_ge(a_lo_ready, 1)
                    freed(pe, u_lo_ready, b)
                    split_product(u_ps, a_hi[:, :], a_lo[:, :], hT_hi[:, :], hT_lo[:, :]).then_inc(u_done, 1)

            def val_product(b):
                if active(b):
                    ready(pe, h_ready, b)
                    if isinstance(b, int) and b == 0:
                        pe.wait_ge(fold_ready, 1)
                    freed(pe, val_ready, b)
                    for j in range(J):
                        m = pe.matmul(val_ps[:, j, :], hT[:, j * P:(j + 1) * P], wvo[:, :], start=True, stop=True)
                    m.then_inc(val_done, 1)

            def s_product(b):
                if active(b):
                    ready(pe, u_hi_ready, b)
                    ready(pe, u_lo_ready, b)
                    if isinstance(b, int) and b == 0:
                        pe.wait_ge(stat_free, 2)
                    freed(pe, pT_ready, b)
                    for j in range(J):
                        rows = slice(j * P, (j + 1) * P)
                        m = split_product(s_ps[:, j, :], uT_hi[:, rows], uT_lo[:, rows], hT_hi[:, :], hT_lo[:, :])
                    m.then_inc(s_done, 1)

            def p_transposes(b):
                if active(b):
                    ready(pe, probs_ready, b)
                    for k in range(J):
                        for j in range(J):
                            t = pe.transpose(s_ps[:, k, j * P:(j + 1) * P], probs[:, j, k * P:(k + 1) * P], ident[:, :])
                    t.then_inc(pT_done, 1)

            def att_product(b):
                if active(b):
                    ready(pe, pT_ready, b)
                    ready(pe, val_ready, b)
                    if isinstance(b, int) and b == 0:
                        pe.wait_ge(rows_ready, 1)
                    freed(pe, x1_ready, b)
                    for j in range(J):
                        for k in range(J):
                            m = pe.matmul(att_ps[:, j, :], probsT[:, k, j * P:(j + 1) * P], vals[:, k, :],
                                          start=(k == 0), stop=(k == J - 1))
                    m.then_inc(att_done, 1)

            def x1_transposes(b):
                if active(b):
                    ready(pe, x1_ready, b)
                    freed(pe, k_ready, b)
                    for j in range(J):
                        t = pe.transpose(x1T_ps[:, j * P:(j + 1) * P], x1[:, j * C:(j + 1) * C], ident[:, :])
                    t.then_inc(x1T_done, 1)

            def kT_product(b):
                if active(b):
                    ready(pe, x1T_hi_ready, b)
                    ready(pe, x1T_lo_ready, b)
                    if isinstance(b, int) and b == 0:
                        pe.wait_ge(w1_split, 1)
                    split_product(kT_ps, w1_hi[:, 1, :], w1_lo[:, 1, :], x1T_hi[:, :], x1T_lo[:, :]).then_inc(kT_done, 1)

            def qv_product(b):
                if active(b):
                    freed(pe, v_ready, b)
                    freed(pe, qb_ready, b)
                    for j in range(J):
                        rows = slice(j * P, (j + 1) * P)
                        m = split_product(qv_ps[:, j, :, :], x1T_hi[:, rows], x1T_lo[:, rows],
                                          w1_hi[:, 0:3:2, :], w1_lo[:, 0:3:2, :])
                    m.then_inc(qv_done, 1)

            def k_transposes(b):
                if active(b):
                    ready(pe, kexp_ready, b)
                    for j in range(J):
                        t = pe.transpose(k_ps[:, j * P:(j + 1) * P], kT_exp[:, j * P:(j + 1) * P], ident[:, :])
                    t.then_inc(k_done, 1)

            def ctx_product(b):
                if active(b):
                    ready(pe, k_ready, b)
                    ready(pe, v_ready, b)
                    freed(pe, y_ready, b)
                    for j in range(J):
                        m = pe.matmul(ctx_ps, v1[:, j, :], k_exp[:, j * C:(j + 1) * C],
                                      start=(j == 0), stop=(j == J - 1))
                    m.then_inc(ctx_done, 1)

            def m_product(b):
                if active(b):
                    ready(pe, ctx_ready, b)
                    pe.matmul(m_ps, ctxT[:, :], wout_sig[:, :], start=True, stop=True).then_inc(m_done, 1)

            def q_transposes(b):
                if active(b):
                    ready(pe, q_ready, b)
                    freed(pe, qT_ready, b)
                    for j in range(J):
                        t = pe.transpose(qT_ps[:, j * P:(j + 1) * P], q_sm[:, j * C:(j + 1) * C], ident[:, :])
                    t.then_inc(qT_done, 1)

            def y_product(b):
                if active(b):
                    ready(pe, qT_ready, b)
                    ready(pe, m_ready, b)
                    for j in range(J):
                        m = pe.matmul(y_ps[:, j * C:(j + 1) * C], qT[:, j * P:(j + 1) * P], m_s[:, :],
                                      start=True, stop=True)
                    m.then_inc(y_done, 1)

            def step(i):
                k_transposes(i - 2)
                att_product(i - 1)
                u_product(i)
                val_product(i)
                if at(i, 0):
                    variances(1)
                ctx_product(i - 2)
                x1_transposes(i - 1)
                s_product(i)
                if at(i, 0):
                    sigmoid_rows()
                if at(i, 0):
                    y_bias_rows()
                m_product(i - 2)
                kT_product(i - 1)
                qv_product(i - 1)
                q_transposes(i - 2)
                p_transposes(i)
                y_product(i - 2)

            pipeline(pe, step)


_INS = ["x", "L0_conv_gn_scale", "L0_conv_gn_bias", "L0_conv_wq", "L0_conv_bq", "L0_conv_wk", "L0_conv_bk",
        "L0_conv_wv", "L0_conv_bv", "L0_conv_wo", "L0_conv_bo", "L1_conv_w_qkv", "L1_conv_b_qkv", "L1_conv_w_out",
        "L1_conv_b_out", "L1_conv_gamma", "L1_conv_beta"]


def kernel(**inputs):
    import numpy as np
    import concourse.bacc as bacc
    from concourse.bass_utils import run_bass_kernel_spmd

    nc = bacc.Bacc("TRN2", target_bir_lowering=False, num_devices=1)
    arrays, args = {}, []
    for name in _INS:
        a = np.ascontiguousarray(inputs[name])
        arrays[f"in_{name}"] = a
        args.append(nc.dram_tensor(f"in_{name}", a.shape, mybir.dt.from_np(a.dtype), kind="ExternalInput").ap())
    y = nc.dram_tensor("out_y", inputs["x"].shape, F32, kind="ExternalOutput").ap()
    build(nc, *args, y)
    r = run_bass_kernel_spmd(nc, [arrays], core_ids=[0])
    return r.results[0]["out_y"]
```

```python
from contextlib import ExitStack

import concourse.bass as bass
from concourse import mybir

F32 = mybir.dt.float32
F32R = mybir.dt.float32r
ALU = mybir.AluOpType
ACT = mybir.ActivationFunctionType
AX_X = mybir.AxisListType.X

GROUPS = 32
HEADS = 8
EPS = 1e-05


def build(nc, x, gn_scale, gn_bias, wq, bq, wk, bk, wv, bv, wo, bo, w_qkv, b_qkv, w_out, b_out, gamma, beta, out):
    B, H, W, C = x.shape
    L = H * W
    P = 128
    J = L // P
    HD = C // HEADS
    GC = C // GROUPS
    SCALE = float(C) ** -0.5
    X_LOADS = [(0, 2), (2, 4), (4, 6), (6, 8)]
    STAT_SETS = [(0, 2), (2, 8)]
    assert C == P and J == 2 and B == 8

    x_d = x.rearrange("b h w c -> b (h w) c").rearrange("b (p j) c -> b p (j c)", j=J)
    y_d = out.rearrange("b h w c -> b (h w) c").rearrange("b (p j) c -> b p (j c)", j=J)

    with ExitStack() as ctx:
        def sb(name, shape, dt=F32):
            return ctx.enter_context(nc.sbuf_tensor(name, shape, dt))

        def ps(name, shape):
            return ctx.enter_context(nc.psum_tensor(name, shape, F32))

        def sem(name):
            return ctx.enter_context(nc.semaphore(name))

        ident = sb("ident", [P, P])
        group_neg = sb("group_neg", [P, P])
        head_mask = sb("head_mask", [P, P])
        wq_s, wk_s, wv_s, wo_s = (sb(n, [P, C]) for n in ("wq_s", "wk_s", "wv_s", "wo_s"))
        w1 = sb("w1", [P, 3, C])
        w1_hi = sb("w1_hi", [P, 3, C], F32R)
        w1_lo = sb("w1_lo", [P, 3, C], F32R)
        wout_s = sb("wout_s", [P, C])
        wout_sig = sb("wout_sig", [P, C])
        VECS = 11
        GNS, GNB, BQ, BV, BO, BQ1, BK1, BV1, BOUT, GAMMA, BETA = range(VECS)
        EARLY = BQ + 1
        vec_rows = sb("vec_rows", [VECS, C])
        turned = sb("turned", [P, 3 * C])
        wqT, wkT, wvT = (turned[:, n * C:(n + 1) * C] for n in range(3))
        vec = sb("vec", [P, VECS])
        ones = sb("ones", [P, P])
        bo_diag, bq1_diag, sig_diag, yb_diag = (sb(n, [P, C]) for n in ("bo_diag", "bq1_diag", "sig_diag", "yb_diag"))
        bq1_b = sb("bq1_b", [P, C])
        a_hi = sb("a_hi", [P, C], F32R)
        a_lo = sb("a_lo", [P, C], F32R)
        a_bias = sb("a_bias", [P, 1])
        wvo = sb("wvo", [P, C])
        bvb = sb("bvb", [P, C])
        bv1b = sb("bv1b", [P, C])
        val_bias = sb("val_bias", [P, C])
        y_bias = sb("y_bias", [P, C])
        sig_e, sig_d, sig, yb_t, yb_u = (sb(n, [P, 1]) for n in ("sig_e", "sig_d", "sig", "yb_t", "yb_u"))
        neg_half = sb("neg_half", [P, B])
        table_load = sb("table_load", [P, 1])

        def row(v, a=1):
            return v.rearrange("(a c) -> a c", a=a)

        LATE_VECTORS = [(BV, row(bv)), (BO, row(bo)), (BQ1, row(b_qkv, 3)), (BOUT, row(b_out)),
                        (GAMMA, gamma.rearrange("a b c d -> (a b c) d")), (BETA, beta.rearrange("a b c d -> (a b c) d"))]

        x_all = sb("x_all", [P, B, J * C])
        xT_all = sb("xT_all", [P, B, L])
        x1b_all = sb("x1b_all", [P, B, J * C])
        y_all = sb("y_all", [P, B, J * C])
        stats = sb("stats", [P, B, 6])
        mv = sb("mv", [P, B, 2])
        dev = sb("dev", [P, B])
        dev2 = sb("dev2", [P, B])
        var_t = sb("var_t", [P, B])
        var_g = sb("var_g", [P, B])
        rstd = sb("rstd", [P, B])
        gn_a = sb("gn_a", [P, B])
        neg_mean = sb("neg_mean", [P, B])
        gn_ba = sb("gn_ba", [P, B])
        gn_b = sb("gn_b", [P, B])

        hT = sb("hT", [P, L])
        hT_hi = sb("hT_hi", [P, L], F32R)
        hT_lo = sb("hT_lo", [P, L], F32R)
        uT_hi = sb("uT_hi", [P, L], F32R)
        uT_lo = sb("uT_lo", [P, L], F32R)
        vals = sb("vals", [P, J, C + 1])
        neg_smax = sb("neg_smax", [P, J])
        probs = sb("probs", [P, J, L])
        probsT = sb("probsT", [P, J, L])
        inv_sum = sb("inv_sum", [P, J])
        x1 = sb("x1", [P, J * C])
        x1T_hi = sb("x1T_hi", [P, L], F32R)
        x1T_lo = sb("x1T_lo", [P, L], F32R)
        neg_kmax = sb("neg_kmax", [P, 1])
        kT_exp = sb("kT_exp", [P, L])
        k_sum = sb("k_sum", [P, 1])
        k_inv = sb("k_inv", [P, 1])
        k_exp = sb("k_exp", [P, J * C])
        v1 = sb("v1", [P, J, C])
        q_b = sb("q_b", [P, J, C])
        q_max = sb("q_max", [P, J * HEADS])
        q_sh = sb("q_sh", [P, J * C])
        q_exp = sb("q_exp", [P, J * C])
        q_sum = sb("q_sum", [P, J * HEADS])
        q_inv = sb("q_inv", [P, J * HEADS])
        q_sm = sb("q_sm", [P, J * C])
        qT = sb("qT", [P, L])
        ctxT = sb("ctxT", [P, C])
        m_s = sb("m_s", [P, C])

        b_u = ps("b_u", [P, 512])
        b_val = ps("b_val", [P, 512])
        b_s = ps("b_s", [P, 512])
        b_att = ps("b_att", [P, 512])
        b_k = ps("b_k", [P, 512])
        b_qv = ps("b_qv", [P, 512])
        b_q = ps("b_q", [P, 512])
        b_y = ps("b_y", [P, 512])
        u_ps = b_u[:, 0:L]
        val_ps = b_val[:, 0:J * C].rearrange("p (j c) -> p j c", j=J)
        s_ps = b_s[:, :].rearrange("p (j l) -> p j l", j=J)
        att_ps = b_att[:, 0:J * (C + 1)].rearrange("p (j c) -> p j c", j=J)
        x1T_ps, kT_ps, k_ps = b_k[:, 0:L], b_k[:, L:2 * L], b_k[:, 0:L]
        qv_ps = b_qv[:, :].rearrange("p (j a c) -> p j a c", j=J, a=2)
        qT_ps = b_q[:, 0:L]
        ctx_ps, m_ps, y_ps = b_y[:, 0:C], b_y[:, C:2 * C], b_y[:, 2 * C:2 * C + J * C]
        XT_BANKS = [b_y, b_q, b_qv, b_k]
        xT_ps = [b[:, 0:L] for b in XT_BANKS]
        wT_ps, vecT_ps, a_ps, fold_ps, rows_ps = b_s, b_att, b_u, b_val, b_q
        val_bias_ps = b_att[:, C:2 * C]
        stat_ps = [b_val, b_y]

        x_in = [sem(f"x_in{n}") for n in range(len(X_LOADS))]
        qk_in, vo_in, w1_in, wout_in, vec_in, gn_in = (
            sem(n) for n in ("qk_in", "vo_in", "w1_in", "wout_in", "vec_in", "gn_in"))
        ones_ready = sem("ones_ready")
        zero_set, pool_set, ident_ready, group_ready, heads_ready, pow_ready = (
            sem(n) for n in ("zero_set", "pool_set", "ident_ready", "group_ready", "heads_ready", "pow_ready"))
        xT_done, stats_done, xT_copied = sem("xT_done"), sem("stats_done"), sem("xT_copied")
        wT_done, wT_copied, vecT_done, vec_ready = sem("wT_done"), sem("wT_copied"), sem("vecT_done"), sem("vec_ready")
        dve_own, pool_own = sem("dve_own"), sem("pool_own")
        stat_free, mean_copied, vecT_free, sig_ready = (
            sem(n) for n in ("stat_free", "mean_copied", "vecT_free", "sig_ready"))
        gnT_done, scales_ready, w1_hi_ready, val_bias_done, val_bias_ready = (
            sem(n) for n in ("gnT_done", "scales_ready", "w1_hi_ready", "val_bias_done", "val_bias_ready"))
        mv_ready, mean_done, dev_ready, var_done, var_ready = (
            sem(n) for n in ("mv_ready", "mean_done", "dev_ready", "var_done", "var_ready"))
        a_done, a_hi_ready, a_lo_ready, diag_ready, fold_done, fold_ready, w1_split = (
            sem(n) for n in ("a_done", "a_hi_ready", "a_lo_ready", "diag_ready", "fold_done", "fold_ready", "w1_split"))
        sig_exp, sig_diag_ready, sig_rows, wout_ready, y_rows_done, rows_ready = (
            sem(n) for n in ("sig_exp", "sig_diag_ready", "sig_rows", "wout_ready", "y_rows_done", "rows_ready"))
        h_ready, h_hi_ready, h_lo_ready = sem("h_ready"), sem("h_hi_ready"), sem("h_lo_ready")
        u_done, u_hi_ready, u_lo_ready = sem("u_done"), sem("u_hi_ready"), sem("u_lo_ready")
        val_done, val_ready = sem("val_done"), sem("val_ready")
        s_done, smax_ready, probs_ready = sem("s_done"), sem("smax_ready"), sem("probs_ready")
        pT_done, pT_ready, att_done = sem("pT_done"), sem("pT_ready"), sem("att_done")
        inv_ready, x1_ready, x1b_ready = sem("inv_ready"), sem("x1_ready"), sem("x1b_ready")
        x1T_done, x1T_hi_ready, x1T_lo_ready = sem("x1T_done"), sem("x1T_hi_ready"), sem("x1T_lo_ready")
        kT_done, kmax_ready, kexp_ready = sem("kT_done"), sem("kmax_ready"), sem("kexp_ready")
        kinv_ready, k_done, k_ready = sem("kinv_ready"), sem("k_done"), sem("k_ready")
        qv_done, v_ready, qb_ready, qmax_ready = sem("qv_done"), sem("v_ready"), sem("qb_ready"), sem("qmax_ready")
        qsh_ready, qexp_ready, qsum_ready, qinv_ready, q_ready = (
            sem(n) for n in ("qsh_ready", "qexp_ready", "qsum_ready", "qinv_ready", "q_ready"))
        qT_done, qT_ready, ctx_done, ctx_ready = sem("qT_done"), sem("qT_ready"), sem("ctx_done"), sem("ctx_ready")
        m_done, m_ready, y_done, y_ready = sem("m_done"), sem("m_ready"), sem("y_done"), sem("y_ready")
        stored = sem("stored")

        def active(b):
            return not isinstance(b, int) or 0 <= b < B

        def ready(eng, signal, b):
            eng.wait_ge(signal, b + 1)

        def freed(eng, signal, b):
            if not isinstance(b, int) or b > 0:
                eng.wait_ge(signal, b)

        def at(b, n):
            return isinstance(b, int) and b == n

        DEPTH = 4

        def pipeline(eng, step):
            for i in range(DEPTH + 1):
                step(i)
            with eng.Fori(DEPTH + 1, B) as i:
                step(i)
            for i in range(B, B + DEPTH):
                step(i)

        own_count = {}

        def own(eng, signal, ins):
            own_count[signal.name] = own_count.get(signal.name, 0) + 1
            ins.then_inc(signal, 1)
            eng.wait_ge(signal, own_count[signal.name])

        block = ctx.enter_context(nc.Block())

        @block.sync
        def _(sp):
            def load_x(n):
                a, b = X_LOADS[n]
                sp.dma_start(x_all[:, a:b, :], x_d[a:b].rearrange("b p f -> p b f")).then_inc(x_in[n], 16)

            def load_vec(r, v, signal):
                sp.dma_start(vec_rows[r:r + v.shape[0], :], v).then_inc(signal, 16)

            load_x(0)
            sp.dma_start(wq_s[:, :], wq).then_inc(qk_in, 16)
            sp.dma_start(wk_s[:, :], wk).then_inc(qk_in, 16)
            load_x(1)
            for r, v in ((GNS, gn_scale), (GNB, gn_bias), (BQ, bq)):
                load_vec(r, row(v), gn_in)
            load_x(2)
            sp.dma_start(wv_s[:, :], wv).then_inc(vo_in, 16)
            sp.dma_start(wo_s[:, :], wo).then_inc(vo_in, 16)
            for r, v in LATE_VECTORS:
                load_vec(r, v, vec_in)
            load_x(3)
            sp.dma_start(w1[:, :, :], w_qkv.rearrange("k (a c) -> k a c", a=3)).then_inc(w1_in, 16)
            sp.dma_start(wout_s[:, :], w_out).then_inc(wout_in, 16)

            with sp.Fori(0, B) as b:
                ready(sp, y_ready, b)
                sp.dma_start(y_d[b], y_all[:, b, :]).then_inc(stored, 16)
            sp.wait_ge(stored, 16 * B)

        @block.gpsimd
        def _(pool):
            pool.memset(ident[:, :], 0.0).then_inc(zero_set, 1)
            pool.wait_ge(zero_set, 1)
            pool.affine_select(out=ident[:, :], in_=ident[:, :], compare_op=ALU.not_equal, fill=1.0, base=0,
                               pattern=[[-1, P]], channel_multiplier=1).then_inc(ident_ready, 1)
            pool.memset(neg_half[:, :], -0.5)
            pool.memset(group_neg[:, :], -1.0 / GC)
            pool.memset(head_mask[:, :], 1.0).then_inc(pool_set, 1)
            n = 1
            for square, side, signal in ((group_neg, GC, group_ready), (head_mask, HD, heads_ready)):
                v = square[:, :].rearrange("p (g s) -> p g s", s=side)
                pool.wait_ge(pool_set, n)
                pool.affine_select(out=v, in_=v, compare_op=ALU.is_ge, fill=0.0, base=0,
                                   pattern=[[-side, C // side], [0, side]],
                                   channel_multiplier=1).then_inc(pool_set, 1)
                n += 1
                pool.wait_ge(pool_set, n)
                pool.affine_select(out=v, in_=v, compare_op=ALU.is_ge, fill=0.0, base=side - 1,
                                   pattern=[[side, C // side], [0, side]],
                                   channel_multiplier=-1).then_inc(signal, 1)
            pool.memset(vals[:, :, C:C + 1], 1.0)
            pool.memset(ones[:, :], 1.0).then_inc(ones_ready, 1)

            def inv_std(n):
                a, b = STAT_SETS[n]
                pool.wait_ge(var_ready, n + 1)
                pool.tensor_tensor(rstd[:, a:b], var_g[:, a:b], neg_half[:, a:b], ALU.pow).then_inc(pow_ready, 1)

            def set_deviations_1():
                a, b = STAT_SETS[1]
                pool.wait_ge(mean_copied, 1)
                pool.wait_ge(mv_ready, b)
                own(pool, pool_own, pool.tensor_tensor(dev[:, a:b], mv[:, a:b, 0], neg_mean[:, a:b], ALU.add))
                own(pool, pool_own, pool.tensor_tensor(dev2[:, a:b], dev[:, a:b], dev[:, a:b], ALU.mult))
                pool.tensor_tensor(var_t[:, a:b], dev2[:, a:b], mv[:, a:b, 1], ALU.add).then_inc(dev_ready, 1)

            def set_scales_1():
                a, b = STAT_SETS[1]
                pool.wait_ge(pow_ready, 2)
                own(pool, pool_own, pool.tensor_tensor(gn_a[:, a:b], rstd[:, a:b],
                                                       vec[:, GNS:GNS + 1].to_broadcast([P, b - a]), ALU.mult))
                own(pool, pool_own, pool.tensor_tensor(gn_ba[:, a:b], neg_mean[:, a:b], gn_a[:, a:b], ALU.mult))
                pool.tensor_tensor(gn_b[:, a:b], gn_ba[:, a:b], vec[:, GNB:GNB + 1].to_broadcast([P, b - a]),
                                   ALU.add).then_inc(scales_ready, 1)

            def spread(out, v):
                return pool.tensor_copy(out[:, :], vec[:, v:v + 1].to_broadcast([P, C]))

            def diagonal(out, column):
                return pool.tensor_tensor(out[:, :], ident[:, :], column.to_broadcast([P, C]), ALU.mult)

            inv_std(0)
            pool.wait_ge(vec_ready, 1)
            diagonal(bo_diag, vec[:, BO:BO + 1])
            spread(bvb, BV).then_inc(diag_ready, 1)
            spread(bv1b, BV1)
            diagonal(bq1_diag, vec[:, BQ1:BQ1 + 1]).then_inc(diag_ready, 1)

            def h_lo(b):
                if active(b):
                    ready(pool, h_hi_ready, b)
                    ready(pool, h_ready, b)
                    freed(pool, s_done, b)
                    if at(b, 0):
                        return
                    pool.tensor_tensor(hT_lo[:, :], hT[:, :], hT_hi[:, :].bitcast(F32),
                                       ALU.subtract).then_inc(h_lo_ready, 1)

            def x1_plus_bias(b):
                if active(b):
                    ready(pool, x1_ready, b)
                    if at(b, 0):
                        pool.wait_ge(rows_ready, 1)
                    pool.tensor_tensor(x1b_all[:, b, :].rearrange("p (j c) -> p j c", j=J),
                                       x1[:, :].rearrange("p (j c) -> p j c", j=J),
                                       y_bias[:, :].unsqueeze(1).to_broadcast([P, J, C]),
                                       ALU.add).then_inc(x1b_ready, 1)

            def q_shift(b):
                if active(b):
                    ready(pool, qmax_ready, b)
                    freed(pool, qexp_ready, b)
                    pool.tensor_tensor(q_sh[:, :].rearrange("p (g d) -> p g d", d=HD),
                                       q_b[:, :, :].rearrange("p j (h d) -> p (j h) d", d=HD),
                                       q_max[:, :].unsqueeze(2).to_broadcast([P, J * HEADS, HD]),
                                       ALU.subtract).then_inc(qsh_ready, 1)

            def q_normal(b):
                if active(b):
                    ready(pool, qinv_ready, b)
                    freed(pool, qT_done, b)
                    pool.tensor_tensor(q_sm[:, :].rearrange("p (g d) -> p g d", d=HD),
                                       q_exp[:, :].rearrange("p (g d) -> p g d", d=HD),
                                       q_inv[:, :].unsqueeze(2).to_broadcast([P, J * HEADS, HD]),
                                       ALU.mult).then_inc(q_ready, 1)

            def step(i):
                h_lo(i)
                if at(i, 0):
                    set_deviations_1()
                if at(i, 1):
                    inv_std(1)
                    set_scales_1()
                q_normal(i - 3)
                x1_plus_bias(i - 2)
                q_shift(i - 2)

            pipeline(pool, step)

        @block.scalar
        def _(act):
            act.wait_ge(ident_ready, 1)
            act.activation(table_load[:, :], ident[:, 0:1], ACT.Exp)

            def xT_copy(b):
                act.wait_ge(stats_done, b + 1)
                act.activation(xT_all[:, b, :], xT_ps[b % len(XT_BANKS)], ACT.Copy).then_inc(xT_copied, 1)

            xT_copy(0)
            xT_copy(1)
            act.wait_ge(wT_done, 1)
            act.activation(turned[:, 0:2 * C], wT_ps[:, 0:2 * C], ACT.Copy).then_inc(wT_copied, 1)
            xT_copy(2)
            act.wait_ge(a_done, 1)
            act.activation(a_hi[:, :], a_ps[:, 0:C], ACT.Copy, scale=SCALE).then_inc(a_hi_ready, 1)
            xT_copy(3)
            act.wait_ge(wT_done, 2)
            act.activation(wvT, wT_ps[:, 2 * C:3 * C], ACT.Copy).then_inc(wT_copied, 1)
            xT_copy(4)

            def fold_copies():
                act.wait_ge(fold_done, 1)
                act.activation(a_bias[:, :], fold_ps[:, 2 * C:2 * C + 1], ACT.Copy, scale=SCALE).then_inc(fold_ready, 1)
                act.activation(wvo[:, :], fold_ps[:, 0:C], ACT.Copy).then_inc(fold_ready, 1)

            def vec_copy():
                act.wait_ge(vecT_done, 1)
                act.activation(vec[:, EARLY:VECS], vecT_ps[:, EARLY:VECS], ACT.Copy).then_inc(vec_ready, 1)
                act.wait_ge(vec_ready, 1)
                act.activation(sig_e[:, :], vec[:, GAMMA:GAMMA + 1], ACT.Exp, scale=-1.0).then_inc(sig_exp, 1)

            def val_bias_copy():
                act.wait_ge(val_bias_done, 1)
                act.activation(val_bias[:, :], val_bias_ps, ACT.Copy).then_inc(val_bias_ready, 1)

            def w1_high():
                act.wait_ge(w1_in, 16)
                act.activation(w1_hi[:, :, :], w1[:, :, :], ACT.Copy).then_inc(w1_hi_ready, 1)

            def sigmoid_diagonals():
                act.wait_ge(sig_ready, 1)
                act.activation(sig_diag[:, :], ident[:, :], ACT.Copy, scale=sig[:, :])
                act.activation(yb_diag[:, :], ident[:, :], ACT.Copy, scale=yb_u[:, :]).then_inc(sig_diag_ready, 1)

            def stat_copies():
                a, b = STAT_SETS[1]
                act.wait_ge(mean_done, 2)
                act.activation(neg_mean[:, a:b], stat_ps[1][:, a:b], ACT.Copy).then_inc(mean_copied, 1)

            def var_copies():
                a, b = STAT_SETS[1]
                act.wait_ge(var_done, 2)
                act.activation(var_g[:, a:b], stat_ps[1][:, B + a:B + b], ACT.Copy, scale=-1.0,
                               bias=EPS).then_inc(var_ready, 1)

            def xT_copies(a, z):
                for b in range(a, z):
                    xT_copy(b)

            def h_high(b):
                if active(b):
                    for n, (first, _) in enumerate(STAT_SETS):
                        if at(b, first):
                            act.wait_ge(scales_ready, n + 1)
                    freed(act, s_done, b)
                    act.activation(hT_hi[:, :], xT_all[:, b, :], ACT.Identity, scale=gn_a[:, bass.ds(b, 1)],
                                   bias=gn_b[:, bass.ds(b, 1)]).then_inc(h_hi_ready, 1)

            def u_high(b):
                if active(b):
                    ready(act, u_done, b)
                    if at(b, 0):
                        act.wait_ge(fold_ready, 1)
                    freed(act, s_done, b)
                    act.activation(uT_hi[:, :], u_ps, ACT.Identity, bias=a_bias[:, :]).then_inc(u_hi_ready, 1)

            def s_exp(b):
                if active(b):
                    ready(act, smax_ready, b)
                    freed(act, pT_done, b)
                    for j in range(J):
                        e = act.activation(probs[:, j, :], s_ps[:, j, :], ACT.Exp, bias=neg_smax[:, j:j + 1])
                    e.then_inc(probs_ready, 1)

            def pT_copy(b):
                if active(b):
                    ready(act, pT_done, b)
                    freed(act, att_done, b)
                    act.activation(probsT[:, :, :], s_ps, ACT.Copy).then_inc(pT_ready, 1)

            def x1T_high(b):
                if active(b):
                    ready(act, x1T_done, b)
                    freed(act, qv_done, b)
                    act.activation(x1T_hi[:, :], x1T_ps, ACT.Copy).then_inc(x1T_hi_ready, 1)

            def k_exp_t(b):
                if active(b):
                    ready(act, kmax_ready, b)
                    freed(act, k_done, b)
                    freed(act, kinv_ready, b)
                    act.activation(kT_exp[:, :], kT_ps, ACT.Exp, bias=neg_kmax[:, :],
                                   accum_out=k_sum[:, :]).then_inc(kexp_ready, 1)

            def v_copy(b):
                if active(b):
                    ready(act, qb_ready, b)
                    freed(act, ctx_done, b)
                    act.activation(v1[:, :, :], qv_ps[:, :, 1, :], ACT.Copy).then_inc(v_ready, 1)

            def k_copy(b):
                if active(b):
                    ready(act, k_done, b)
                    freed(act, ctx_done, b)
                    act.activation(k_exp[:, :], k_ps, ACT.Copy).then_inc(k_ready, 1)

            def q_exp_n(b):
                if active(b):
                    ready(act, qsh_ready, b)
                    freed(act, q_ready, b)
                    act.activation(q_exp[:, :], q_sh[:, :], ACT.Exp).then_inc(qexp_ready, 1)

            def m_copy(b):
                if active(b):
                    ready(act, m_done, b)
                    ready(act, kinv_ready, b)
                    freed(act, y_done, b)
                    act.activation(m_s[:, :], m_ps, ACT.Copy, scale=k_inv[:, :]).then_inc(m_ready, 1)

            def qT_copy(b):
                if active(b):
                    ready(act, qT_done, b)
                    freed(act, y_done, b)
                    act.activation(qT[:, :], qT_ps, ACT.Copy).then_inc(qT_ready, 1)

            def step(i):
                h_high(i)
                if at(i, 0):
                    fold_copies()
                x1T_high(i - 2)
                s_exp(i - 1)
                if at(i - 1, 0):
                    var_copies()
                    w1_high()
                pT_copy(i - 1)
                k_exp_t(i - 2)
                m_copy(i - 3)
                u_high(i)
                if at(i, 0):
                    vec_copy()
                    xT_copies(5, B)
                    val_bias_copy()
                    stat_copies()
                if at(i, 1):
                    sigmoid_diagonals()
                qT_copy(i - 3)
                k_copy(i - 2)
                v_copy(i - 2)
                q_exp_n(i - 2)

            pipeline(act, step)

        @block.vector
        def _(dve):
            def channel_stats(b):
                dve.wait_ge(xT_done, b + 1)
                dve.bn_stats(stats[:, b, :], xT_ps[b % len(XT_BANKS)]).then_inc(stats_done, 1)

            def set_means(n):
                a, b = STAT_SETS[n]
                dve.wait_ge(stats_done, b)
                for k in range(a, b):
                    dve.bn_aggr(mv[:, k, :], stats[:, k, :]).then_inc(mv_ready, 1)

            def set_deviations(n):
                a, b = STAT_SETS[n]
                dve.wait_ge(mean_done, n + 1)
                own(dve, dve_own, dve.tensor_tensor(dev[:, a:b], mv[:, a:b, 0], stat_ps[n][:, a:b], ALU.add))
                own(dve, dve_own, dve.tensor_tensor(dev2[:, a:b], dev[:, a:b], dev[:, a:b], ALU.mult))
                dve.tensor_tensor(var_t[:, a:b], dev2[:, a:b], mv[:, a:b, 1], ALU.add).then_inc(dev_ready, 1)

            def set_variances(n):
                a, b = STAT_SETS[n]
                dve.wait_ge(var_done, n + 1)
                dve.tensor_scalar(var_g[:, a:b], stat_ps[n][:, B + a:B + b], -1.0, EPS,
                                  ALU.mult, ALU.add).then_inc(var_ready, 1)
                dve.tensor_copy(neg_mean[:, a:b], stat_ps[n][:, a:b]).then_inc(stat_free, 1)

            def set_scales(n):
                a, b = STAT_SETS[n]
                dve.wait_ge(pow_ready, n + 1)
                own(dve, dve_own, dve.tensor_scalar(gn_a[:, a:b], rstd[:, a:b], vec[:, GNS:GNS + 1], None, ALU.mult))
                own(dve, dve_own, dve.tensor_tensor(gn_ba[:, a:b], neg_mean[:, a:b], gn_a[:, a:b], ALU.mult))
                dve.tensor_scalar(gn_b[:, a:b], gn_ba[:, a:b], vec[:, GNB:GNB + 1], None,
                                  ALU.add).then_inc(scales_ready, 1)

            def more_stats(a, z):
                for b in range(a, z):
                    channel_stats(b)

            more_stats(0, 2)
            set_means(0)
            channel_stats(2)
            set_deviations(0)
            channel_stats(3)
            set_variances(0)
            dve.wait_ge(gnT_done, 1)
            dve.tensor_copy(vec[:, 0:EARLY], vecT_ps[:, 0:EARLY]).then_inc(vecT_free, 1)
            dve.wait_ge(a_hi_ready, 1)
            dve.scalar_tensor_tensor(out=a_lo[:, :], in0=a_ps[:, 0:C], scalar=SCALE, in1=a_hi[:, :].bitcast(F32),
                                     op0=ALU.mult, op1=ALU.subtract).then_inc(a_lo_ready, 1)
            channel_stats(4)
            dve.wait_ge(vecT_free, 1)
            set_scales(0)

            def h_norm(b):
                if active(b):
                    for n, (first, _) in enumerate(STAT_SETS):
                        if at(b, first):
                            dve.wait_ge(scales_ready, n + 1)
                    freed(dve, val_done, b)
                    freed(dve, h_lo_ready, b)
                    dve.tensor_scalar(hT[:, :], xT_all[:, b, :], gn_a[:, bass.ds(b, 1)], gn_b[:, bass.ds(b, 1)],
                                      ALU.mult, ALU.add).then_inc(h_ready, 1)
                    if at(b, 0):
                        dve.wait_ge(h_hi_ready, 1)
                        dve.wait_ge(h_ready, 1)
                        dve.tensor_tensor(hT_lo[:, :], hT[:, :], hT_hi[:, :].bitcast(F32),
                                          ALU.subtract).then_inc(h_lo_ready, 1)

            def u_low(b):
                if active(b):
                    ready(dve, u_hi_ready, b)
                    freed(dve, s_done, b)
                    dve.scalar_tensor_tensor(out=uT_lo[:, :], in0=u_ps, scalar=a_bias[:, :],
                                             in1=uT_hi[:, :].bitcast(F32), op0=ALU.add,
                                             op1=ALU.subtract).then_inc(u_lo_ready, 1)

            def val_copy(b):
                if active(b):
                    ready(dve, val_done, b)
                    freed(dve, att_done, b)
                    if at(b, 0):
                        dve.wait_ge(val_bias_ready, 1)
                    dve.tensor_tensor(vals[:, :, 0:C], val_ps, val_bias[:, :].unsqueeze(1).to_broadcast([P, J, C]),
                                      ALU.add).then_inc(val_ready, 1)

            def s_max(b):
                if active(b):
                    ready(dve, s_done, b)
                    freed(dve, probs_ready, b)
                    dve.tensor_reduce(neg_smax[:, :], s_ps, AX_X, ALU.max, negate=True).then_inc(smax_ready, 1)

            def x1_rows(b):
                if active(b):
                    ready(dve, att_done, b)
                    dve.reciprocal(inv_sum[:, :], att_ps[:, :, C]).then_inc(inv_ready, 1)
                    ready(dve, inv_ready, b)
                    freed(dve, x1T_done, b)
                    freed(dve, x1b_ready, b)
                    for j in range(J):
                        r = dve.scalar_tensor_tensor(out=x1[:, j * C:(j + 1) * C], in0=att_ps[:, j, 0:C],
                                                     scalar=inv_sum[:, j:j + 1],
                                                     in1=x_all[:, b, j * C:(j + 1) * C],
                                                     op0=ALU.mult, op1=ALU.add)
                    r.then_inc(x1_ready, 1)

            def x1T_low(b):
                if active(b):
                    ready(dve, x1T_hi_ready, b)
                    freed(dve, qv_done, b)
                    dve.tensor_tensor(x1T_lo[:, :], x1T_ps, x1T_hi[:, :].bitcast(F32),
                                      ALU.subtract).then_inc(x1T_lo_ready, 1)

            def k_max(b):
                if active(b):
                    ready(dve, kT_done, b)
                    freed(dve, kexp_ready, b)
                    dve.tensor_reduce(neg_kmax[:, :], kT_ps, AX_X, ALU.max, negate=True).then_inc(kmax_ready, 1)

            def k_recip(b):
                if active(b):
                    ready(dve, kexp_ready, b)
                    freed(dve, m_ready, b)
                    dve.reciprocal(k_inv[:, :], k_sum[:, :]).then_inc(kinv_ready, 1)

            def q_bias(b):
                if active(b):
                    ready(dve, qv_done, b)
                    freed(dve, qsh_ready, b)
                    dve.tensor_tensor(q_b[:, :, :], qv_ps[:, :, 0, :],
                                      bq1_b[:, :].unsqueeze(1).to_broadcast([P, J, C]), ALU.add).then_inc(qb_ready, 1)

            def q_maxima(b):
                if active(b):
                    ready(dve, qb_ready, b)
                    dve.tensor_reduce(q_max[:, :], q_b[:, :, :].rearrange("p j (h d) -> p (j h) d", d=HD),
                                      AX_X, ALU.max).then_inc(qmax_ready, 1)

            def q_sums(b):
                if active(b):
                    ready(dve, qexp_ready, b)
                    dve.tensor_reduce(q_sum[:, :], q_exp[:, :].rearrange("p (g d) -> p g d", d=HD),
                                      AX_X, ALU.add).then_inc(qsum_ready, 1)
                    ready(dve, qsum_ready, b)
                    freed(dve, q_ready, b)
                    dve.reciprocal(q_inv[:, :], q_sum[:, :]).then_inc(qinv_ready, 1)

            def ctx_mask(b):
                if active(b):
                    ready(dve, ctx_done, b)
                    freed(dve, m_done, b)
                    if at(b, 0):
                        dve.wait_ge(heads_ready, 1)
                    dve.tensor_tensor(ctxT[:, :], ctx_ps, head_mask[:, :], ALU.mult).then_inc(ctx_ready, 1)

            def y_rows(b):
                if active(b):
                    ready(dve, y_done, b)
                    ready(dve, x1b_ready, b)
                    dve.tensor_tensor(y_all[:, b, :], y_ps, x1b_all[:, b, :], ALU.add).then_inc(y_ready, 1)

            def w1_low():
                dve.wait_ge(w1_in, 16)
                dve.wait_ge(w1_hi_ready, 1)
                dve.tensor_tensor(w1_lo[:, :, :], w1[:, :, :], w1_hi[:, :, :].bitcast(F32),
                                   ALU.subtract).then_inc(w1_split, 1)

            def set_sigmoid():
                dve.wait_ge(sig_exp, 1)
                own(dve, dve_own, dve.tensor_scalar(sig_d[:, :], sig_e[:, :], 1.0, None, ALU.add))
                own(dve, dve_own, dve.reciprocal(sig[:, :], sig_d[:, :]))
                own(dve, dve_own, dve.tensor_tensor(yb_t[:, :], vec[:, BOUT:BOUT + 1], sig[:, :], ALU.mult))
                dve.tensor_tensor(yb_u[:, :], yb_t[:, :], vec[:, BETA:BETA + 1], ALU.add).then_inc(sig_ready, 1)

            def set_wout():
                dve.wait_ge(wout_in, 16)
                dve.wait_ge(sig_rows, 1)
                dve.tensor_copy(bq1_b[:, :], rows_ps[:, C:2 * C])
                dve.tensor_tensor(wout_sig[:, :], wout_s[:, :], rows_ps[:, 0:C], ALU.mult).then_inc(wout_ready, 1)

            def set_y_bias():
                dve.wait_ge(y_rows_done, 1)
                dve.tensor_copy(y_bias[:, :], rows_ps[:, 2 * C:3 * C]).then_inc(rows_ready, 1)

            def step(i):
                s_max(i - 1)
                if at(i - 1, 1):
                    set_wout()
                y_rows(i - 4)
                x1T_low(i - 2)
                h_norm(i)
                q_sums(i - 3)
                ctx_mask(i - 3)
                k_max(i - 2)
                if at(i - 2, 0):
                    set_y_bias()
                val_copy(i - 1)
                if at(i - 1, 0):
                    set_sigmoid()
                    w1_low()
                q_bias(i - 2)
                q_maxima(i - 2)
                u_low(i)
                if at(i, 0):
                    more_stats(5, B)
                    set_means(1)
                k_recip(i - 2)
                x1_rows(i - 1)

            pipeline(dve, step)

        @block.tensor
        def _(pe):
            def x_transposes(b):
                for n, (a, z) in enumerate(X_LOADS):
                    if b == a:
                        pe.wait_ge(x_in[n], 16)
                if b >= len(XT_BANKS):
                    pe.wait_ge(xT_copied, b - len(XT_BANKS) + 1)
                for j in range(J):
                    t = pe.transpose(xT_ps[b % len(XT_BANKS)][:, j * P:(j + 1) * P], x_all[:, b, j * C:(j + 1) * C], ident[:, :])
                t.then_inc(xT_done, 1)

            def means(n):
                a, b = STAT_SETS[n]
                pe.wait_ge(mv_ready, b)
                if n:
                    pe.wait_ge(xT_copied, B)
                pe.matmul(stat_ps[n][:, a:b], group_neg[:, :], mv[:, a:b, 0], start=True, stop=True).then_inc(mean_done, 1)

            def variances(n):
                a, b = STAT_SETS[n]
                pe.wait_ge(dev_ready, n + 1)
                pe.matmul(stat_ps[n][:, B + a:B + b], group_neg[:, :], var_t[:, a:b],
                          start=True, stop=True).then_inc(var_done, 1)

            pe.wait_ge(ident_ready, 1)
            x_transposes(0)
            x_transposes(1)
            pe.wait_ge(qk_in, 32)
            pe.transpose(wT_ps[:, 0:C], wq_s[:, :], ident[:, :])
            pe.transpose(wT_ps[:, C:2 * C], wk_s[:, :], ident[:, :]).then_inc(wT_done, 1)
            x_transposes(2)
            pe.wait_ge(group_ready, 1)
            means(0)
            pe.wait_ge(wT_copied, 1)
            pe.matmul(a_ps[:, 0:C], wqT, wkT, start=True, stop=True).then_inc(a_done, 1)
            x_transposes(3)
            variances(0)
            pe.wait_ge(gn_in, 16 * EARLY)
            pe.transpose(vecT_ps[:, 0:EARLY], vec_rows[0:EARLY, :], ident[0:EARLY, 0:EARLY]).then_inc(gnT_done, 1)
            x_transposes(4)
            pe.wait_ge(vo_in, 32)
            pe.wait_ge(stat_free, 1)
            pe.transpose(wT_ps[:, 2 * C:3 * C], wv_s[:, :], ident[:, :]).then_inc(wT_done, 1)
            pe.wait_ge(vecT_free, 1)
            pe.matmul(fold_ps[:, 2 * C:2 * C + 1], wkT, vec[:, BQ:BQ + 1], start=True, stop=True)
            pe.wait_ge(wT_copied, 2)
            pe.matmul(fold_ps[:, 0:C], wvT, wo_s[:, :], start=True, stop=True).then_inc(fold_done, 1)

            def vec_transpose():
                pe.wait_ge(vec_in, 16 * len(LATE_VECTORS))
                pe.transpose(vecT_ps[:, 0:VECS], vec_rows[:, :], ident[0:VECS, 0:VECS]).then_inc(vecT_done, 1)

            def val_bias_rows():
                pe.wait_ge(diag_ready, 1)
                pe.wait_ge(ones_ready, 1)
                pe.matmul(val_bias_ps, bvb[:, :], wo_s[:, :], start=True, stop=False)
                pe.matmul(val_bias_ps, ones[:, :], bo_diag[:, :], start=False, stop=True).then_inc(val_bias_done, 1)

            def sigmoid_rows():
                pe.wait_ge(diag_ready, 2)
                pe.wait_ge(sig_diag_ready, 1)
                pe.matmul(rows_ps[:, 0:C], ones[:, :], sig_diag[:, :], start=True, stop=True)
                pe.matmul(rows_ps[:, C:2 * C], ones[:, :], bq1_diag[:, :], start=True, stop=True).then_inc(sig_rows, 1)

            def y_bias_rows():
                pe.wait_ge(wout_ready, 1)
                pe.matmul(rows_ps[:, 2 * C:3 * C], bv1b[:, :], wout_sig[:, :], start=True, stop=False)
                pe.matmul(rows_ps[:, 2 * C:3 * C], ones[:, :], yb_diag[:, :], start=False, stop=True).then_inc(y_rows_done, 1)

            def split_product(out_ps, w_hi, w_lo, m_hi, m_lo):
                pe.matmul(out_ps, w_hi, m_hi, start=True, stop=False)
                pe.matmul(out_ps, w_hi, m_lo, start=False, stop=False)
                return pe.matmul(out_ps, w_lo, m_hi, start=False, stop=True)

            def u_product(b):
                if active(b):
                    ready(pe, h_lo_ready, b)
                    ready(pe, h_hi_ready, b)
                    if at(b, 0):
                        pe.wait_ge(a_lo_ready, 1)
                    freed(pe, u_lo_ready, b)
                    split_product(u_ps, a_hi[:, :], a_lo[:, :], hT_hi[:, :], hT_lo[:, :]).then_inc(u_done, 1)

            def val_product(b):
                if active(b):
                    ready(pe, h_ready, b)
                    if at(b, 0):
                        pe.wait_ge(fold_ready, 2)
                    freed(pe, val_ready, b)
                    for j in range(J):
                        m = pe.matmul(val_ps[:, j, :], hT[:, j * P:(j + 1) * P], wvo[:, :], start=True, stop=True)
                    m.then_inc(val_done, 1)

            def s_product(b):
                if active(b):
                    ready(pe, u_lo_ready, b)
                    ready(pe, u_hi_ready, b)
                    freed(pe, pT_ready, b)
                    for j in range(J):
                        rows = slice(j * P, (j + 1) * P)
                        m = split_product(s_ps[:, j, :], uT_hi[:, rows], uT_lo[:, rows], hT_hi[:, :], hT_lo[:, :])
                    m.then_inc(s_done, 1)

            def p_transposes(b):
                if active(b):
                    ready(pe, probs_ready, b)
                    for k in range(J):
                        for j in range(J):
                            t = pe.transpose(s_ps[:, k, j * P:(j + 1) * P], probs[:, j, k * P:(k + 1) * P], ident[:, :])
                    t.then_inc(pT_done, 1)

            def att_product(b):
                if active(b):
                    ready(pe, pT_ready, b)
                    ready(pe, val_ready, b)
                    freed(pe, x1_ready, b)
                    for j in range(J):
                        for k in range(J):
                            m = pe.matmul(att_ps[:, j, :], probsT[:, k, j * P:(j + 1) * P], vals[:, k, :],
                                          start=(k == 0), stop=(k == J - 1))
                    m.then_inc(att_done, 1)

            def x1_transposes(b):
                if active(b):
                    ready(pe, x1_ready, b)
                    freed(pe, k_ready, b)
                    for j in range(J):
                        t = pe.transpose(x1T_ps[:, j * P:(j + 1) * P], x1[:, j * C:(j + 1) * C], ident[:, :])
                    t.then_inc(x1T_done, 1)

            def kT_product(b):
                if active(b):
                    ready(pe, x1T_lo_ready, b)
                    ready(pe, x1T_hi_ready, b)
                    if at(b, 0):
                        pe.wait_ge(w1_split, 1)
                    split_product(kT_ps, w1_hi[:, 1, :], w1_lo[:, 1, :], x1T_hi[:, :], x1T_lo[:, :]).then_inc(kT_done, 1)

            def qv_product(b):
                if active(b):
                    freed(pe, v_ready, b)
                    freed(pe, qb_ready, b)
                    for j in range(J):
                        rows = slice(j * P, (j + 1) * P)
                        m = split_product(qv_ps[:, j, :, :], x1T_hi[:, rows], x1T_lo[:, rows],
                                          w1_hi[:, 0:3:2, :], w1_lo[:, 0:3:2, :])
                    m.then_inc(qv_done, 1)

            def k_transposes(b):
                if active(b):
                    ready(pe, kexp_ready, b)
                    for j in range(J):
                        t = pe.transpose(k_ps[:, j * P:(j + 1) * P], kT_exp[:, j * P:(j + 1) * P], ident[:, :])
                    t.then_inc(k_done, 1)

            def ctx_product(b):
                if active(b):
                    ready(pe, v_ready, b)
                    ready(pe, k_ready, b)
                    if at(b, 0):
                        pe.wait_ge(var_ready, 2)
                    freed(pe, y_ready, b)
                    for j in range(J):
                        m = pe.matmul(ctx_ps, v1[:, j, :], k_exp[:, j * C:(j + 1) * C],
                                      start=(j == 0), stop=(j == J - 1))
                    m.then_inc(ctx_done, 1)

            def m_product(b):
                if active(b):
                    ready(pe, ctx_ready, b)
                    pe.matmul(m_ps, ctxT[:, :], wout_sig[:, :], start=True, stop=True).then_inc(m_done, 1)

            def q_transposes(b):
                if active(b):
                    ready(pe, q_ready, b)
                    if at(b, 0):
                        pe.wait_ge(rows_ready, 1)
                    freed(pe, qT_ready, b)
                    for j in range(J):
                        t = pe.transpose(qT_ps[:, j * P:(j + 1) * P], q_sm[:, j * C:(j + 1) * C], ident[:, :])
                    t.then_inc(qT_done, 1)

            def y_product(b):
                if active(b):
                    ready(pe, qT_ready, b)
                    ready(pe, m_ready, b)
                    for j in range(J):
                        m = pe.matmul(y_ps[:, j * C:(j + 1) * C], qT[:, j * P:(j + 1) * P], m_s[:, :],
                                      start=True, stop=True)
                    m.then_inc(y_done, 1)

            def step(i):
                y_product(i - 4)
                x1_transposes(i - 2)
                val_product(i - 1)
                if at(i - 1, 0):
                    variances(1)
                ctx_product(i - 3)
                kT_product(i - 2)
                if at(i - 2, 0):
                    y_bias_rows()
                p_transposes(i - 1)
                qv_product(i - 2)
                m_product(i - 3)
                u_product(i)
                if at(i, 0):
                    vec_transpose()
                    x_transposes(5)
                    x_transposes(6)
                    x_transposes(7)
                q_transposes(i - 3)
                att_product(i - 1)
                k_transposes(i - 2)
                s_product(i)
                if at(i, 0):
                    val_bias_rows()
                    means(1)
                if at(i, 1):
                    sigmoid_rows()

            pipeline(pe, step)


_INS = ["x", "L0_conv_gn_scale", "L0_conv_gn_bias", "L0_conv_wq", "L0_conv_bq", "L0_conv_wk", "L0_conv_bk",
        "L0_conv_wv", "L0_conv_bv", "L0_conv_wo", "L0_conv_bo", "L1_conv_w_qkv", "L1_conv_b_qkv", "L1_conv_w_out",
        "L1_conv_b_out", "L1_conv_gamma", "L1_conv_beta"]


def kernel(**inputs):
    import numpy as np
    import concourse.bacc as bacc
    from concourse.bass_utils import run_bass_kernel_spmd

    nc = bacc.Bacc("TRN2", target_bir_lowering=False, num_devices=1)
    arrays, args = {}, []
    for name in _INS:
        a = np.ascontiguousarray(inputs[name])
        arrays[f"in_{name}"] = a
        args.append(nc.dram_tensor(f"in_{name}", a.shape, mybir.dt.from_np(a.dtype), kind="ExternalInput").ap())
    y = nc.dram_tensor("out_y", inputs["x"].shape, F32, kind="ExternalOutput").ap()
    build(nc, *args, y)
    r = run_bass_kernel_spmd(nc, [arrays], core_ids=[0])
    return r.results[0]["out_y"]
```
